# Optimizing a Trainium2 kernel written in Bass

```python
import numpy as np
import jax
import jax.numpy as jnp

def _softmax(x, axis=-1):
    return jax.nn.softmax(x, axis=axis)

def _gelu(x):
    return jax.nn.gelu(x, approximate=True)

def _silu(x):
    return jax.nn.silu(x)

def _sigmoid(x):
    return jax.nn.sigmoid(x)

def _layernorm(x, axis=-1, eps=1e-05):
    m = jnp.mean(x, axis=axis, keepdims=True)
    v = jnp.var(x, axis=axis, keepdims=True)
    return (x - m) / jnp.sqrt(v + eps)

def _scatter_add(tgt, idx, src, axis=0):
    return tgt.at[idx].add(src)

def _segment_sum(src, seg, n):
    return jax.ops.segment_sum(src, seg, n)
kernel_name = 'mk_xattn_seq_d2_seqx_r4_72e423'

def setup_inputs(seed: int=0):
    np.random.seed(seed)
    _w = jnp.asarray

    def _rec_inputs():
        import jax
        import jax.numpy as jnp
        _rk = jax.random.key(seed)
        x = -0.0002928 + 1 * jax.random.normal(jax.random.fold_in(_rk, 1), (1, 2048, 256), jnp.float32)
        _lenS = 2048 - jax.random.randint(jax.random.fold_in(_rk, 7), (1,), 0, max(1, 2048 // 4) + 1, jnp.int32)
        _lenS2 = 1601 - jax.random.randint(jax.random.fold_in(_rk, 8), (1,), 0, max(1, 1601 // 4) + 1, jnp.int32)
        _ctx_1024P = jax.random.normal(jax.random.fold_in(_rk, 11), (1, 16, 256), jnp.float32)
        _ctx_1024c = jax.random.dirichlet(jax.random.fold_in(_rk, 511), 0.3 * jnp.ones((16,), jnp.float32), (1, 1601))
        _ctx_1024t = jnp.einsum('bsk,bkd->bsd', _ctx_1024c, _ctx_1024P)
        _ctx_1024t = _ctx_1024t * jax.lax.rsqrt(jnp.mean(jnp.square(_ctx_1024t)) + 1e-12) * 0.953939
        ctx_1024 = 0.000227908 + 0.99994 * (_ctx_1024t + 0.3 * jax.random.normal(jax.random.fold_in(_rk, 611), (1, 1601, 256), jnp.float32))
        return (x, ctx_1024)
    x, ctx_1024 = _rec_inputs()

    def _L0_xattn_setup():
        import jax, jax.numpy as jnp
        import numpy as np
        B, S, SC, D, H, DFF = (4, 256, 64, 256, 16, 1024)
        DK = D // H
        EPS = 1e-05

        def _layernorm(x, g, b):
            mu = jnp.mean(x, axis=-1, keepdims=True)
            var = jnp.mean(jnp.square(x - mu), axis=-1, keepdims=True)
            return (x - mu) * jax.lax.rsqrt(var + EPS) * g + b

        def _attend(q, k, v):

            def heads(t):
                b, s, _ = t.shape
                return t.reshape(b, s, H, DK).transpose(0, 2, 1, 3)
            qh, kh, vh = (heads(q), heads(k), heads(v))
            scores = jnp.einsum('bhqd,bhkd->bhqk', qh, kh) / jnp.sqrt(jnp.float32(DK))
            w = jax.nn.softmax(scores, axis=-1)
            ctx = jnp.einsum('bhqk,bhkd->bhqd', w, vh)
            b, _, sq, _ = ctx.shape
            return ctx.transpose(0, 2, 1, 3).reshape(b, sq, D)
        key = jax.random.key(seed)
        ks = jax.random.split(key, 16)
        sc = 0.02
        n = lambda k, shp: jax.random.normal(k, shp, jnp.float32) * sc
        z = lambda shp: jnp.zeros(shp, jnp.float32)
        o = lambda shp: jnp.ones(shp, jnp.float32)
        return {'x': jax.random.normal(ks[0], (B, S, D), jnp.float32), 'condition': jax.random.normal(ks[1], (B, SC, D), jnp.float32), 'in_proj_w': n(ks[2], (3 * D, D)), 'in_proj_b': z((3 * D,)), 'out_proj_w': n(ks[3], (D, D)), 'out_proj_b': z((D,)), 'cq_w': n(ks[4], (D, D)), 'cq_b': z((D,)), 'ck_w': n(ks[5], (D, D)), 'ck_b': z((D,)), 'cv_w': n(ks[6], (D, D)), 'cv_b': z((D,)), 'co_w': n(ks[7], (D, D)), 'co_b': z((D,)), 'ff1_w': n(ks[8], (DFF, D)), 'ff1_b': z((DFF,)), 'ff2_w': n(ks[9], (D, DFF)), 'ff2_b': z((D,)), 'ln1_g': o((D,)), 'ln1_b': z((D,)), 'ln2_g': o((D,)), 'ln2_b': z((D,)), 'ln3_g': o((D,)), 'ln3_b': z((D,))}
    _L0_xattn_all = _L0_xattn_setup()
    _L0_xattn_in = {k: v for k, v in _L0_xattn_all.items() if k in ('in_proj_w', 'in_proj_b', 'out_proj_w', 'out_proj_b', 'cq_w', 'cq_b', 'ck_w', 'ck_b', 'cv_w', 'cv_b', 'co_w', 'co_b', 'ff1_w', 'ff1_b', 'ff2_w', 'ff2_b', 'ln1_g', 'ln1_b', 'ln2_g', 'ln2_b', 'ln3_g', 'ln3_b')}
    del _L0_xattn_all

    def _L1_xattn_setup():
        import jax, jax.numpy as jnp
        import numpy as np
        EPS = 1e-06
        H = 16

        def _ln(x):
            mu = jnp.mean(x, axis=-1, keepdims=True)
            var = jnp.mean(jnp.square(x - mu), axis=-1, keepdims=True)
            return (x - mu) / jnp.sqrt(var + EPS)

        def _mod(x, shift, scale):
            return x * (1.0 + scale[:, None, :]) + shift[:, None, :]

        def _heads(x, qkv_w, qkv_b):
            B, N, C = x.shape
            hd = C // H
            qkv = (x @ qkv_w + qkv_b).reshape(B, N, 3, H, hd).transpose(2, 0, 3, 1, 4)
            return (qkv[0], qkv[1], qkv[2])

        def _attend(q, k, v):
            sc = q.shape[-1] ** (-0.5)
            a = jax.nn.softmax(jnp.einsum('bhnd,bhmd->bhnm', q, k) * sc, axis=-1)
            o = jnp.einsum('bhnm,bhmd->bhnd', a, v)
            B, h, N, hd = o.shape
            return o.transpose(0, 2, 1, 3).reshape(B, N, h * hd)

        def _mha(x, qkv_w, qkv_b, proj_w, proj_b):
            q, k, v = _heads(x, qkv_w, qkv_b)
            return _attend(q, k, v) @ proj_w + proj_b
        key = jax.random.key(seed)
        ks = jax.random.split(key, 16)
        B, T, D = (2, 512, 256)
        Dh = 4 * D
        s = 0.02
        return {'x': jax.random.normal(ks[0], (B, T, D), jnp.float32), 'c': jax.random.normal(ks[1], (B, 2, D), jnp.float32), 'attn_qkv_w': jax.random.normal(ks[2], (D, 3 * D), jnp.float32) * s, 'attn_qkv_b': jnp.zeros((3 * D,), jnp.float32), 'attn_proj_w': jax.random.normal(ks[3], (D, D), jnp.float32) * s, 'attn_proj_b': jnp.zeros((D,), jnp.float32), 'crs_qkv_w': jax.random.normal(ks[4], (D, 3 * D), jnp.float32) * s, 'crs_qkv_b': jnp.zeros((3 * D,), jnp.float32), 'crs_proj_w': jax.random.normal(ks[5], (D, D), jnp.float32) * s, 'crs_proj_b': jnp.zeros((D,), jnp.float32), 'mlp_fc1_w': jax.random.normal(ks[6], (D, Dh), jnp.float32) * s, 'mlp_fc1_b': jnp.zeros((Dh,), jnp.float32), 'mlp_fc2_w': jax.random.normal(ks[7], (Dh, D), jnp.float32) * s, 'mlp_fc2_b': jnp.zeros((D,), jnp.float32), 'ada_w': jax.random.normal(ks[8], (D, 9 * D), jnp.float32) * s, 'ada_b': jnp.zeros((9 * D,), jnp.float32)}
    _L1_xattn_all = _L1_xattn_setup()
    _L1_xattn_in = {k: v for k, v in _L1_xattn_all.items() if k in ('attn_qkv_w', 'attn_qkv_b', 'attn_proj_w', 'attn_proj_b', 'crs_qkv_w', 'crs_qkv_b', 'crs_proj_w', 'crs_proj_b', 'mlp_fc1_w', 'mlp_fc1_b', 'mlp_fc2_w', 'mlp_fc2_b', 'ada_w', 'ada_b')}
    del _L1_xattn_all
    return {'x': x, 'ctx_1024': ctx_1024, 'L0_xattn_in_proj_w': _L0_xattn_in['in_proj_w'], 'L0_xattn_in_proj_b': _L0_xattn_in['in_proj_b'], 'L0_xattn_out_proj_w': _L0_xattn_in['out_proj_w'], 'L0_xattn_out_proj_b': _L0_xattn_in['out_proj_b'], 'L0_xattn_cq_w': _L0_xattn_in['cq_w'], 'L0_xattn_cq_b': _L0_xattn_in['cq_b'], 'L0_xattn_ck_w': _L0_xattn_in['ck_w'], 'L0_xattn_ck_b': _L0_xattn_in['ck_b'], 'L0_xattn_cv_w': _L0_xattn_in['cv_w'], 'L0_xattn_cv_b': _L0_xattn_in['cv_b'], 'L0_xattn_co_w': _L0_xattn_in['co_w'], 'L0_xattn_co_b': _L0_xattn_in['co_b'], 'L0_xattn_ff1_w': _L0_xattn_in['ff1_w'], 'L0_xattn_ff1_b': _L0_xattn_in['ff1_b'], 'L0_xattn_ff2_w': _L0_xattn_in['ff2_w'], 'L0_xattn_ff2_b': _L0_xattn_in['ff2_b'], 'L0_xattn_ln1_g': _L0_xattn_in['ln1_g'], 'L0_xattn_ln1_b': _L0_xattn_in['ln1_b'], 'L0_xattn_ln2_g': _L0_xattn_in['ln2_g'], 'L0_xattn_ln2_b': _L0_xattn_in['ln2_b'], 'L0_xattn_ln3_g': _L0_xattn_in['ln3_g'], 'L0_xattn_ln3_b': _L0_xattn_in['ln3_b'], 'L1_xattn_attn_qkv_w': _L1_xattn_in['attn_qkv_w'], 'L1_xattn_attn_qkv_b': _L1_xattn_in['attn_qkv_b'], 'L1_xattn_attn_proj_w': _L1_xattn_in['attn_proj_w'], 'L1_xattn_attn_proj_b': _L1_xattn_in['attn_proj_b'], 'L1_xattn_crs_qkv_w': _L1_xattn_in['crs_qkv_w'], 'L1_xattn_crs_qkv_b': _L1_xattn_in['crs_qkv_b'], 'L1_xattn_crs_proj_w': _L1_xattn_in['crs_proj_w'], 'L1_xattn_crs_proj_b': _L1_xattn_in['crs_proj_b'], 'L1_xattn_mlp_fc1_w': _L1_xattn_in['mlp_fc1_w'], 'L1_xattn_mlp_fc1_b': _L1_xattn_in['mlp_fc1_b'], 'L1_xattn_mlp_fc2_w': _L1_xattn_in['mlp_fc2_w'], 'L1_xattn_mlp_fc2_b': _L1_xattn_in['mlp_fc2_b'], 'L1_xattn_ada_w': _L1_xattn_in['ada_w'], 'L1_xattn_ada_b': _L1_xattn_in['ada_b']}

def reference(x, ctx_1024, L0_xattn_in_proj_w, L0_xattn_in_proj_b, L0_xattn_out_proj_w, L0_xattn_out_proj_b, L0_xattn_cq_w, L0_xattn_cq_b, L0_xattn_ck_w, L0_xattn_ck_b, L0_xattn_cv_w, L0_xattn_cv_b, L0_xattn_co_w, L0_xattn_co_b, L0_xattn_ff1_w, L0_xattn_ff1_b, L0_xattn_ff2_w, L0_xattn_ff2_b, L0_xattn_ln1_g, L0_xattn_ln1_b, L0_xattn_ln2_g, L0_xattn_ln2_b, L0_xattn_ln3_g, L0_xattn_ln3_b, L1_xattn_attn_qkv_w, L1_xattn_attn_qkv_b, L1_xattn_attn_proj_w, L1_xattn_attn_proj_b, L1_xattn_crs_qkv_w, L1_xattn_crs_qkv_b, L1_xattn_crs_proj_w, L1_xattn_crs_proj_b, L1_xattn_mlp_fc1_w, L1_xattn_mlp_fc1_b, L1_xattn_mlp_fc2_w, L1_xattn_mlp_fc2_b, L1_xattn_ada_w, L1_xattn_ada_b):
    import jax
    import jax.numpy as jnp

    def _L0_xattn_ref(x, condition, in_proj_w, in_proj_b, out_proj_w, out_proj_b, cq_w, cq_b, ck_w, ck_b, cv_w, cv_b, co_w, co_b, ff1_w, ff1_b, ff2_w, ff2_b, ln1_g, ln1_b, ln2_g, ln2_b, ln3_g, ln3_b):
        import jax, jax.numpy as jnp
        import numpy as np
        B, S, SC, D, H, DFF = (4, 256, 64, 256, 16, 1024)
        DK = D // H
        EPS = 1e-05

        def _layernorm(x, g, b):
            mu = jnp.mean(x, axis=-1, keepdims=True)
            var = jnp.mean(jnp.square(x - mu), axis=-1, keepdims=True)
            return (x - mu) * jax.lax.rsqrt(var + EPS) * g + b

        def _attend(q, k, v):

            def heads(t):
                b, s, _ = t.shape
                return t.reshape(b, s, H, DK).transpose(0, 2, 1, 3)
            qh, kh, vh = (heads(q), heads(k), heads(v))
            scores = jnp.einsum('bhqd,bhkd->bhqk', qh, kh) / jnp.sqrt(jnp.float32(DK))
            w = jax.nn.softmax(scores, axis=-1)
            ctx = jnp.einsum('bhqk,bhkd->bhqd', w, vh)
            b, _, sq, _ = ctx.shape
            return ctx.transpose(0, 2, 1, 3).reshape(b, sq, D)
        residual = x
        h = _layernorm(x, ln1_g, ln1_b)
        qkv = h @ in_proj_w.T + in_proj_b
        q, k, v = jnp.split(qkv, 3, axis=-1)
        sa = _attend(q, k, v) @ out_proj_w.T + out_proj_b
        x = residual + sa
        residual = x
        h = _layernorm(x, ln2_g, ln2_b)
        q = h @ cq_w.T + cq_b
        k = condition @ ck_w.T + ck_b
        v = condition @ cv_w.T + cv_b
        ca = _attend(q, k, v) @ co_w.T + co_b
        x = residual + ca
        residual = x
        h = _layernorm(x, ln3_g, ln3_b)
        h = jax.nn.gelu(h @ ff1_w.T + ff1_b, approximate=False)
        h = h @ ff2_w.T + ff2_b
        return residual + h

    def _L1_xattn_ref(x, c, attn_qkv_w, attn_qkv_b, attn_proj_w, attn_proj_b, crs_qkv_w, crs_qkv_b, crs_proj_w, crs_proj_b, mlp_fc1_w, mlp_fc1_b, mlp_fc2_w, mlp_fc2_b, ada_w, ada_b):
        import jax, jax.numpy as jnp
        import numpy as np
        EPS = 1e-06
        H = 16

        def _ln(x):
            mu = jnp.mean(x, axis=-1, keepdims=True)
            var = jnp.mean(jnp.square(x - mu), axis=-1, keepdims=True)
            return (x - mu) / jnp.sqrt(var + EPS)

        def _mod(x, shift, scale):
            return x * (1.0 + scale[:, None, :]) + shift[:, None, :]

        def _heads(x, qkv_w, qkv_b):
            B, N, C = x.shape
            hd = C // H
            qkv = (x @ qkv_w + qkv_b).reshape(B, N, 3, H, hd).transpose(2, 0, 3, 1, 4)
            return (qkv[0], qkv[1], qkv[2])

        def _attend(q, k, v):
            sc = q.shape[-1] ** (-0.5)
            a = jax.nn.softmax(jnp.einsum('bhnd,bhmd->bhnm', q, k) * sc, axis=-1)
            o = jnp.einsum('bhnm,bhmd->bhnd', a, v)
            B, h, N, hd = o.shape
            return o.transpose(0, 2, 1, 3).reshape(B, N, h * hd)

        def _mha(x, qkv_w, qkv_b, proj_w, proj_b):
            q, k, v = _heads(x, qkv_w, qkv_b)
            return _attend(q, k, v) @ proj_w + proj_b
        mod = jax.nn.silu(c) @ ada_w + ada_b
        sh_msa, sc_msa, g_msa, sh_mca, sc_mca, g_mca, sh_mlp, sc_mlp, g_mlp = jnp.split(mod, 9, axis=2)
        B, T, D = x.shape
        h = T // 2
        x0, x1 = (x[:, :h], x[:, h:])
        x0 = x0 + g_msa[:, 0][:, None, :] * _mha(_mod(_ln(x0), sh_msa[:, 0], sc_msa[:, 0]), attn_qkv_w, attn_qkv_b, attn_proj_w, attn_proj_b)
        x1 = x1 + g_msa[:, 1][:, None, :] * _mha(_mod(_ln(x1), sh_msa[:, 1], sc_msa[:, 1]), attn_qkv_w, attn_qkv_b, attn_proj_w, attn_proj_b)
        xm = _mod(_ln(x0), sh_mca[:, 0], sc_mca[:, 0])
        ym = _mod(_ln(x1), sh_mca[:, 1], sc_mca[:, 1])
        qx, kx, vx = _heads(xm, crs_qkv_w, crs_qkv_b)
        qy, ky, vy = _heads(ym, crs_qkv_w, crs_qkv_b)
        ox = _attend(qx, ky, vy) @ crs_proj_w + crs_proj_b
        oy = _attend(qy, kx, vx) @ crs_proj_w + crs_proj_b
        x = x + jnp.concatenate((g_mca[:, 0][:, None, :] * ox, g_mca[:, 1][:, None, :] * oy), axis=1)

        def mlp(z):
            return jax.nn.gelu(z @ mlp_fc1_w + mlp_fc1_b, approximate=True) @ mlp_fc2_w + mlp_fc2_b
        m0 = mlp(_mod(_ln(x[:, :h]), sh_mlp[:, 0], sc_mlp[:, 0]))
        m1 = mlp(_mod(_ln(x[:, h:]), sh_mlp[:, 1], sc_mlp[:, 1]))
        x = x + jnp.concatenate((g_mlp[:, 0][:, None, :] * m0, g_mlp[:, 1][:, None, :] * m1), axis=1)
        return x
    x = _L0_xattn_ref(x, ctx_1024, L0_xattn_in_proj_w, L0_xattn_in_proj_b, L0_xattn_out_proj_w, L0_xattn_out_proj_b, L0_xattn_cq_w, L0_xattn_cq_b, L0_xattn_ck_w, L0_xattn_ck_b, L0_xattn_cv_w, L0_xattn_cv_b, L0_xattn_co_w, L0_xattn_co_b, L0_xattn_ff1_w, L0_xattn_ff1_b, L0_xattn_ff2_w, L0_xattn_ff2_b, L0_xattn_ln1_g, L0_xattn_ln1_b, L0_xattn_ln2_g, L0_xattn_ln2_b, L0_xattn_ln3_g, L0_xattn_ln3_b)
    x = _L1_xattn_ref(x, ctx_1024, L1_xattn_attn_qkv_w, L1_xattn_attn_qkv_b, L1_xattn_attn_proj_w, L1_xattn_attn_proj_b, L1_xattn_crs_qkv_w, L1_xattn_crs_qkv_b, L1_xattn_crs_proj_w, L1_xattn_crs_proj_b, L1_xattn_mlp_fc1_w, L1_xattn_mlp_fc1_b, L1_xattn_mlp_fc2_w, L1_xattn_mlp_fc2_b, L1_xattn_ada_w, L1_xattn_ada_b)
    return x

_drawn_inputs = setup_inputs


def setup_inputs(seed=0):
    import zlib

    import numpy as np

    out = dict(_drawn_inputs(seed))
    spreads = {'L0_xattn_in_proj_b': (0.0, 0.1),
     'L0_xattn_out_proj_b': (0.0, 0.1),
     'L0_xattn_cq_b': (0.0, 0.8),
     'L0_xattn_ck_b': (0.0, 0.8),
     'L0_xattn_cv_b': (0.0, 0.271),
     'L0_xattn_co_b': (0.0, 0.1),
     'L0_xattn_ff1_b': (0.0, 0.1),
     'L0_xattn_ff2_b': (0.0, 0.1),
     'L0_xattn_ln1_g': (1.0, 0.6),
     'L0_xattn_ln1_b': (0.0, 0.8),
     'L0_xattn_ln2_g': (1.0, 0.6),
     'L0_xattn_ln2_b': (0.0, 0.8),
     'L0_xattn_ln3_g': (1.0, 0.6),
     'L0_xattn_ln3_b': (0.0, 0.679),
     'L1_xattn_attn_qkv_b': (0.0, 0.8),
     'L1_xattn_attn_proj_b': (0.0, 0.8),
     'L1_xattn_crs_qkv_b': (0.0, 0.8),
     'L1_xattn_crs_proj_b': (0.0, 0.355),
     'L1_xattn_mlp_fc1_b': (0.0, 0.8),
     'L1_xattn_mlp_fc2_b': (0.0, 0.351),
     'L1_xattn_ada_b': (0.0, 0.387)}
    factors = {'L0_xattn_in_proj_w': 5.37,
     'L0_xattn_cq_w': 8.0,
     'L0_xattn_ck_w': 8.0,
     'L1_xattn_attn_qkv_w': 8.0,
     'L1_xattn_attn_proj_w': 8.0,
     'L1_xattn_crs_qkv_w': 8.0,
     'L1_xattn_crs_proj_w': 5.581}
    for name, (base, spread) in spreads.items():
        noise = np.random.default_rng([zlib.crc32(name.encode()), seed]).standard_normal(out[name].shape)
        drawn = base * np.exp(spread * noise) if base else spread * noise
        out[name] = jnp.asarray(drawn.astype(out[name].dtype))
    for name, factor in factors.items():
        out[name] = (out[name] * factor).astype(out[name].dtype)
    return out
```

```python
import concourse.bass as bass
from concourse import mybir
from contextlib import ExitStack

FP32 = mybir.dt.float32
BF16 = mybir.dt.bfloat16
ALU = mybir.AluOpType
ACT = mybir.ActivationFunctionType
AX = mybir.AxisListType
ds = bass.ds

P = 128
S = 2048
D = 256
KC = D // P
T = S // P
BLK = 512
NBLK = S // BLK
TB = BLK // P
SC = 1601
H = 16
DK = D // H
HG = 4
G = H // HG
GW = HG * DK
F = 1024
FC = F // P
SCALE = 0.25

Q_PARTS = (0, 0, 0, 1, 1, 2)
K_PARTS = (0, 1, 2, 0, 1, 0)
KQ = len(Q_PARTS) * DK
KM = 3


class Attention:

    def __init__(self, name, stages, queries, keys):
        self.name = name
        self.J = stages
        self.NQ = queries
        self.NK = keys
        self.NB = queries // BLK
        self.U = stages * self.NB
        self.KT = (keys + P - 1) // P
        self.KW = [min(P, keys - P * k) for k in range(self.KT)]
        self.NKB = (keys + BLK - 1) // BLK
        self.KBW = [min(BLK, keys - BLK * k) for k in range(self.NKB)]
        self.NI = HG * TB
        self.NA = self.NI * self.NKB
        self.EV = 2 * (self.KT + 1)
        self.M_STEP = self.KT - 2
        self.A_STEPS = max(1, self.KT - 2)
        self.VC = 4
        self.NVC = (self.KT + self.VC - 1) // self.VC


def build(nc, x, ctxT, w, out):
    ctx = ExitStack()
    with ctx:
        def sb(name, shape, dt=FP32, stack=ctx):
            return stack.enter_context(nc.sbuf_tensor(name, shape, dt))

        def lasting_sem(name):
            return ctx.enter_context(nc.semaphore(name))

        class Stage:
            last = None

            def __init__(self):
                self.stack = ExitStack()
                self.sems = []
                self.before = Stage.last
                Stage.last = self

            def sem(self, name):
                self.sems.append(self.stack.enter_context(nc.semaphore(name)))
                return self.sems[-1]

            def clear_before(self, pool):
                for s in self.before.sems if self.before else ():
                    pool.sem_clear(s)

            def end(self):
                if self.before:
                    self.before.stack.close()

        def dram(name, shape, dt=FP32):
            return nc.dram_tensor(name, shape, dt, kind="Internal").ap()

        xs = sb("xs", [P, T, D])
        hT = sb("hT", [P, KC, S])
        cT = sb("cT", [P, KC, SC])
        v_all = sb("v_all", [P, 64, GW])
        xmid = v_all[:, :, :].rearrange("p (t k) f -> p t (k f)", t=T)
        ident = sb("ident", [P, P])
        identb = sb("identb", [P, P], BF16)
        wq = sb("wq", [P, KC, 3 * D])
        wo = sb("wo", [P, KC, D])
        wcq = sb("wcq", [P, KC, 3 * D])
        wco = sb("wco", [P, KC, D])
        cols = sb("cols", [P, w["cols"].shape[1]])
        rows = sb("rows", [P, w["rows"].shape[0], D])
        shift = sb("shift", [P, 12, 2])
        gate = sb("gate", [P, 2, 3, D])
        gbias = sb("gbias", [P, 2, 3, D])
        eps = sb("eps", [P, 2])
        ps = ctx.enter_context(nc.psum_tensor("ps", [P, 8, BLK], FP32))

        COL = w["col_at"]
        ROW = w["row_at"]

        attn = [Attention("a0", G, S, S), Attention("a1", G, S, SC),
                Attention("a2", 2 * G, S // 2, S // 2), Attention("a3", 2 * G, S // 2, S // 2)]
        q_dram = [dram(f"q_parts{a.name}", [a.J, GW, 3, a.NQ], BF16) for a in attn]
        k_dram = [dram(f"k_parts{a.name}", [a.J, GW, 3, a.NK], BF16) for a in attn]
        o_dram = [dram(f"attended{a.name}", [a.J, P, a.NQ]) for a in attn]
        r_dram = [dram(f"inverse_sums{a.name}", [a.J, HG, a.NQ]) for a in attn]

        ld = {n: lasting_sem("ld_" + n) for n in ("x", "ctx", "small", "wq", "wo", "wcq", "wco", "wf1", "wf2", "ada",
                                          "wq2", "wo2", "wcq2", "wco2", "wf12", "wf22")}
        s_id = lasting_sem("identities_made")

        def chunked(ap):
            return ap.rearrange("(c p) n -> p c n", p=P)

        stage = Stage()
        sem = stage.sem
        s_silu, s_modp, s_mod, s_gatep, s_gate = (sem(n) for n in ("silu_done", "mod_ready", "mod_done", "gate_ready", "gate_done"))
        with ExitStack() as tmp:
            ada = sb("ada", [P, KC, 9 * D], FP32, tmp)
            sil = sb("sil", [P, KC, 2], FP32, tmp)
            silr = sb("silr", [P, KC, 2, P], FP32, tmp)
            zero = sb("zero", [P, P], FP32, tmp)
            blk = tmp.enter_context(nc.Block())
            VECS = (0, 1, 3, 4, 6, 7)
            GATES = (2, 5, 8)

            @blk.sync
            def _(eng):
                eng.dma_start(cT[:, :, :], chunked(ctxT)).then_inc(ld["ctx"], 16)
                eng.dma_start(cols[:, :], w["cols"]).then_inc(ld["small"], 16)
                eng.dma_start(rows[:, :, :], w["rows"].partition_broadcast(P)).then_inc(ld["small"], 16)
                eng.dma_start(xs[:, :, :], x.rearrange("(t p) d -> p t d", p=P)).then_inc(ld["x"], 16)
                eng.dma_start(wq[:, :, :], chunked(w["in_proj"])).then_inc(ld["wq"], 16)
                eng.dma_start(wo[:, :, :], chunked(w["out_proj"])).then_inc(ld["wo"], 16)
                for i, n in enumerate(("cq", "ck", "cv")):
                    eng.dma_start(wcq[:, :, i * D:(i + 1) * D], chunked(w[n])).then_inc(ld["wcq"], 16)
                eng.dma_start(wco[:, :, :], chunked(w["co"])).then_inc(ld["wco"], 16)

            @blk.gpsimd
            def _(eng):
                stage.clear_before(eng)
                eng.memset(ident[:, :], 0.0).then_inc(s_id, 1)
                eng.memset(identb[:, :], 0.0).then_inc(s_id, 1)
                eng.memset(zero[:, :], 0.0).then_inc(s_id, 1)
                eng.memset(eps[:, 0:1], 1e-5).then_inc(s_id, 1)
                eng.memset(eps[:, 1:2], 1e-6).then_inc(s_id, 1)
                eng.wait_ge(s_id, 2)
                for m in (ident, identb):
                    eng.affine_select(out=m[:, :], in_=m[:, :], compare_op=ALU.not_equal, fill=1.0,
                                      base=0, pattern=[[-1, P]], channel_multiplier=1).then_inc(s_id, 1)

            @blk.scalar
            def _(eng):
                eng.dma_start(ada[:, :, :], chunked(w["ada"])).then_inc(ld["ada"], 16)
                eng.wait_ge(ld["ctx"], 16)
                eng.activation(sil[:, :, :], cT[:, :, 0:2], ACT.Silu).then_inc(s_silu, 1)
                eng.wait_ge(s_silu, 1)
                eng.wait_ge(s_id, 3)
                for kc in range(KC):
                    for half in range(2):
                        eng.activation(silr[:, kc, half, :], zero[:, :], ACT.Identity,
                                       bias=sil[:, kc, half:half + 1]).then_inc(s_silu, 1)

            @blk.tensor
            def _(eng):
                eng.wait_ge(ld["ada"], 16)
                eng.wait_ge(s_silu, 1)
                for i, v in enumerate(VECS):
                    for c in range(KC):
                        for kc in range(KC):
                            last = eng.matmul(ps[:, 0, 4 * i + 2 * c:4 * i + 2 * c + 2],
                                              ada[:, kc, v * D + c * P:v * D + (c + 1) * P], sil[:, kc, :],
                                              start=(kc == 0), stop=(kc == KC - 1))
                last.then_inc(s_modp, 1)
                eng.wait_ge(s_silu, 1 + 2 * KC)
                for half in range(2):
                    for k, v in enumerate(GATES):
                        for kc in range(KC):
                            last = eng.matmul(ps[:, 1 + half * 3 + k, 0:D], silr[:, kc, half, :],
                                              ada[:, kc, v * D:(v + 1) * D], start=(kc == 0), stop=(kc == KC - 1))
                last.then_inc(s_gatep, 1)

            @blk.vector
            def _(eng):
                eng.wait_ge(ld["small"], 32)
                eng.wait_ge(s_modp, 1)
                for i, v in enumerate(VECS):
                    for c in range(KC):
                        n = 2 * i + c
                        b = COL["ada_b"] + 2 * v + c
                        eng.tensor_scalar(shift[:, n, :], ps[:, 0, 2 * n:2 * n + 2], cols[:, b:b + 1], float(i % 2),
                                          ALU.add, ALU.add).then_inc(s_mod, 1)
                eng.wait_ge(s_gatep, 1)
                for half in range(2):
                    for k in range(3):
                        eng.tensor_tensor(gate[:, half, k, :], ps[:, 1 + half * 3 + k, 0:D],
                                          rows[:, ROW["gate"] + k, :], ALU.add).then_inc(s_gate, 1)
                eng.wait_ge(s_gate, 6)
                for half in range(2):
                    for k in range(3):
                        eng.tensor_tensor(gbias[:, half, k, :], gate[:, half, k, :],
                                          rows[:, ROW["out2"] + k, :], ALU.mult).then_inc(s_gate, 1)

        stage.end()

        def norm_stage(tag, e, scale_at, shift_at, make_jobs, mlp=None, src=xs):
            stage = Stage()
            sem = stage.sem
            s_stat, s_var, s_std, s_rstd = (sem(n + tag) for n in ("bn_stats_done", "variance_done", "std_done", "rstd_done"))
            s_h, s_tp, s_hT = (sem(n + tag) for n in ("normed_ready", "transposed_ready", "hT_ready"))
            s_pj, s_pjfree = sem("projected_ready" + tag), sem("projection_bank_free" + tag)
            with ExitStack() as tmp:
                st = sb("st" + tag, [P, T, 6], FP32, tmp)
                mv = sb("mv" + tag, [P, T, 2], FP32, tmp)
                std = sb("std" + tag, [P, T], FP32, tmp)
                rstd = sb("rstd" + tag, [P, T], FP32, tmp)
                h = sb("h" + tag, [P, T, D], FP32, tmp)
                NPART = 4
                if mlp is None:
                    jobs = make_jobs()
                    parts = sb("parts" + tag, [P, NPART, 3, BLK], BF16, tmp)
                    rest = sb("rest" + tag, [P, NPART, BLK], FP32, tmp)
                    s_q1, s_q2, s_q3 = (sem(n + tag) for n in ("part1_done", "part2_done", "part3_done"))
                    s_stored = [sem(f"parts_stored{i}" + tag) for i in range(NPART)]
                else:
                    fcol, func, gated, (w1, w2), (s_w1, s_w2), final = mlp
                    wf1 = sb("wf1" + tag, [P, KC, F], FP32, tmp)
                    wf2 = sb("wf2" + tag, [P, FC, D], FP32, tmp)
                    hid = sb("hid" + tag, [P, 2, FC, BLK], FP32, tmp)
                    s_hid, s_y, s_xb, s_xo, s_out = (sem(n + tag) for n in
                                                     ("hidden_ready", "mlp_out_ready", "bias_added", "residual_done", "stored"))
                blk = tmp.enter_context(nc.Block())

                def normalise(eng):
                    eng.wait_ge(ld["x"], 16)
                    eng.wait_ge(ld["small"], 32)
                    for b in range(NBLK):
                        for t in range(b * TB, (b + 1) * TB):
                            eng.bn_stats(st[:, t, :], src[:, t, :]).then_inc(s_stat, 1)
                        for t in range(b * TB, (b + 1) * TB):
                            eng.wait_ge(s_stat, t + 1)
                            eng.bn_aggr(mv[:, t, :], st[:, t, :]).then_inc(s_var, 1)
                    for b in range(NBLK):
                        a, z = b * TB, (b + 1) * TB
                        eng.wait_ge(s_std, b + 1)
                        eng.reciprocal(rstd[:, a:z], std[:, a:z]).then_inc(s_rstd, 1)
                        eng.wait_ge(s_rstd, b + 1)
                        for t in range(a, z):
                            eng.tensor_scalar(h[:, t, :], src[:, t, :], mv[:, t, 0:1], rstd[:, t:t + 1],
                                              ALU.subtract, ALU.mult).then_inc(s_h, 1)

                def deviations(eng):
                    eng.wait_ge(s_id, 7)
                    for b in range(NBLK):
                        a, z = b * TB, (b + 1) * TB
                        eng.wait_ge(s_var, z)
                        eng.activation(std[:, a:z], mv[:, a:z, 1], ACT.Sqrt, bias=eps[:, e:e + 1]).then_inc(s_std, 1)

                def transposes(eng, b):
                    if b >= 2:
                        eng.wait_ge(s_hT, KC * (b - 1))
                    for kc in range(KC):
                        for t in range(TB):
                            if kc == 0:
                                eng.wait_ge(s_h, b * TB + t + 1)
                            last = eng.transpose(ps[:, 2 * (b % 2) + kc, t * P:(t + 1) * P],
                                                 h[:, b * TB + t, kc * P:(kc + 1) * P], ident[:, :])
                        last.then_inc(s_tp, 1)

                def affine(eng, b):
                    half = b // (NBLK // 2)
                    for kc in range(KC):
                        eng.wait_ge(s_tp, KC * b + kc + 1)
                        eng.activation(hT[:, kc, b * BLK:(b + 1) * BLK], ps[:, 2 * (b % 2) + kc, :], ACT.Identity,
                                       bias=shift_at(kc, half), scale=scale_at(kc, half)).then_inc(s_hT, 1)

                if mlp is None:
                    def bank(n):
                        return 4 + n % 4

                    qk_index, count = [], 0
                    for job in jobs:
                        qk_index.append(count)
                        count += job[0] == "qk"

                    @blk.vector
                    def _(eng):
                        normalise(eng)
                        for n, job in enumerate(jobs):
                            i = qk_index[n]
                            if job[0] == "qk":
                                _, _, _, col, _, _, nt, _ = job
                                buf = i % NPART
                                if i >= NPART:
                                    eng.wait_ge(s_q3, i - NPART + 1)
                                eng.wait_ge(s_q1, i + 1)
                                eng.scalar_tensor_tensor(out=rest[:, buf, 0:nt], in0=ps[:, bank(n), 0:nt],
                                                         scalar=cols[:, col:col + 1], in1=parts[:, buf, 0, 0:nt],
                                                         op0=ALU.add, op1=ALU.subtract).then_inc(s_pjfree, 1)
                                eng.wait_ge(s_pjfree, n + 1)
                                eng.tensor_copy(parts[:, buf, 1, 0:nt], rest[:, buf, 0:nt]).then_inc(s_q2, 1)
                            else:
                                _, _, _, row, tt, nt, at, _ = job
                                eng.wait_ge(s_pj, n + 1)
                                eng.tensor_tensor(at(v_all, nt), ps[0:nt, bank(n), 0:D].rearrange("p (g f) -> p g f", g=G),
                                                  rows[0:nt, row, :].rearrange("p (g f) -> p g f", g=G),
                                                  ALU.add).then_inc(s_pjfree, 1)

                    @blk.scalar
                    def _(eng):
                        eng.wait_ge(ld["small"], 32)
                        deviations(eng)
                        done = -1
                        for n, job in enumerate(jobs):
                            b = job[-1]
                            while b is not None and done < min(b + 1, NBLK - 1):
                                done += 1
                                affine(eng, done)
                            if job[0] == "qk":
                                _, _, _, col, _, _, nt, _ = job
                                i = qk_index[n]
                                buf = i % NPART
                                if i >= NPART:
                                    eng.wait_ge(s_stored[buf], 16 * (i // NPART))
                                eng.wait_ge(s_pj, n + 1)
                                eng.activation(parts[:, buf, 0, 0:nt], ps[:, bank(n), 0:nt], ACT.Identity,
                                               bias=cols[:, col:col + 1]).then_inc(s_q1, 1)

                    @blk.gpsimd
                    def _(eng):
                        stage.clear_before(eng)
                        for i, job in enumerate(j for j in jobs if j[0] == "qk"):
                            nt, buf = job[6], i % NPART
                            eng.wait_ge(s_q2, i + 1)
                            if i >= NPART:
                                eng.wait_ge(s_stored[buf], 16 * (i // NPART))
                            eng.tensor_tensor(parts[:, buf, 2, 0:nt], rest[:, buf, 0:nt], parts[:, buf, 1, 0:nt],
                                              ALU.subtract).then_inc(s_q3, 1)

                    @blk.sync
                    def _(eng):
                        stored = [0] * NPART
                        for i, job in enumerate(j for j in jobs if j[0] == "qk"):
                            _, _, _, _, dst, (_, t0), nt, _ = job
                            buf = i % NPART
                            eng.wait_ge(s_q3, i + 1)
                            eng.dma_start(dst[:, :, t0:t0 + nt], parts[:, buf, :, 0:nt]).then_inc(s_stored[buf], 16)
                            stored[buf] += 16
                        for buf in range(NPART):
                            if stored[buf]:
                                eng.wait_ge(s_stored[buf], stored[buf])

                    @blk.tensor
                    def _(eng):
                        eng.wait_ge(s_id, 7)
                        moved = -1
                        waited = set()
                        for n, job in enumerate(jobs):
                            b = job[-1]
                            if b is not None:
                                while moved < min(b + 1, NBLK - 1):
                                    moved += 1
                                    transposes(eng, moved)
                                eng.wait_ge(s_hT, KC * (b + 1))
                            for name, value in job[2][1]:
                                if name not in waited:
                                    waited.add(name)
                                    eng.wait_ge(ld[name], value)
                            if n >= 4:
                                eng.wait_ge(s_pjfree, n - 3)
                            wt = job[2][0]
                            for kc in range(KC):
                                if job[0] == "qk":
                                    last = eng.matmul(ps[:, bank(n), 0:job[6]], wt(kc), job[1][:, kc, job[5][0]:job[5][0] + job[6]],
                                                      start=(kc == 0), stop=(kc == KC - 1))
                                else:
                                    t0 = job[4] * P
                                    last = eng.matmul(ps[0:job[5], bank(n), 0:D], job[1][:, kc, t0:t0 + job[5]], wt(kc),
                                                      start=(kc == 0), stop=(kc == KC - 1))
                            last.then_inc(s_pj, 1)
                else:

                    @blk.vector
                    def _(eng):
                        normalise(eng)
                        eng.wait_ge(s_xb, 1)
                        for b in range(NBLK):
                            for j in range(2):
                                n = 2 * b + j
                                t = b * TB + 2 * j
                                eng.wait_ge(s_y, n + 1)
                                y = ps[:, 6 + n % 2, :].rearrange("p (t d) -> p t d", t=2)
                                if gated:
                                    g = gate[:, b // 2, 2:3, :].to_broadcast([P, 2, D])
                                    eng.tensor_tensor(h[:, t:t + 2, :], y, g, ALU.mult).then_inc(s_pjfree, 1)
                                    eng.wait_ge(s_pjfree, n + 1)
                                    eng.tensor_tensor(xs[:, t:t + 2, :], xs[:, t:t + 2, :], h[:, t:t + 2, :],
                                                      ALU.add).then_inc(s_xo, 1)
                                else:
                                    eng.tensor_tensor(xs[:, t:t + 2, :], y, xs[:, t:t + 2, :], ALU.add).then_inc(s_xo, 1)

                    @blk.gpsimd
                    def _(eng):
                        stage.clear_before(eng)
                        eng.wait_ge(s_h, T)
                        eng.wait_ge(s_tp, KC * NBLK)
                        for half in range(2):
                            r = gbias[:, half, 2:3, :] if gated else rows[:, ROW["ff2_b"]:ROW["ff2_b"] + 1, :]
                            v = xs[:, half * T // 2:(half + 1) * T // 2, :]
                            ins = eng.tensor_tensor(v, v, r.to_broadcast([P, T // 2, D]), ALU.add)
                        ins.then_inc(s_xb, 1)

                    @blk.scalar
                    def _(eng):
                        eng.wait_ge(ld["small"], 32)
                        deviations(eng)
                        affine(eng, 0)
                        for b in range(NBLK):
                            if b + 1 < NBLK:
                                affine(eng, b + 1)
                            for f in range(FC):
                                n = b * FC + f
                                if f == 0 and b >= 2:
                                    eng.wait_ge(s_y, 2 * (b - 1))
                                eng.wait_ge(s_pj, n + 1)
                                eng.activation(hid[:, b % 2, f, :], ps[:, 4 + n % 2, :], func,
                                               bias=cols[:, fcol + f:fcol + f + 1]).then_inc(s_hid, 1)

                    @blk.tensor
                    def _(eng):
                        eng.wait_ge(s_id, 7)
                        transposes(eng, 0)
                        eng.wait_ge(ld[s_w1], 16)
                        for b in range(NBLK + 1):
                            if b < NBLK:
                                if b + 1 < NBLK:
                                    transposes(eng, b + 1)
                                eng.wait_ge(s_hT, KC * (b + 1))
                            for f in range(FC if b < NBLK else 0):
                                n = b * FC + f
                                if n >= 2:
                                    eng.wait_ge(s_hid, n - 1)
                                for kc in range(KC):
                                    last = eng.matmul(ps[:, 4 + n % 2, :], wf1[:, kc, f * P:(f + 1) * P],
                                                      hT[:, kc, b * BLK:(b + 1) * BLK], start=(kc == 0), stop=(kc == KC - 1))
                                last.then_inc(s_pj, 1)
                            if b == 0:
                                eng.wait_ge(ld[s_w2], 16)
                                continue
                            eng.wait_ge(s_hid, b * FC)
                            for j in range(2):
                                n = 2 * (b - 1) + j
                                if n >= 2:
                                    eng.wait_ge(s_pjfree if gated else s_xo, n - 1)
                                for t in range(2):
                                    for f in range(FC):
                                        last = eng.matmul(ps[:, 6 + n % 2, t * D:(t + 1) * D],
                                                          hid[:, (b - 1) % 2, f, (2 * j + t) * P:(2 * j + t + 1) * P],
                                                          wf2[:, f, :], start=(f == 0), stop=(f == FC - 1))
                                last.then_inc(s_y, 1)

                    @blk.sync
                    def _(eng):
                        eng.dma_start(wf1[:, :, :], chunked(w1)).then_inc(ld[s_w1], 16)
                        eng.dma_start(wf2[:, :, :], chunked(w2)).then_inc(ld[s_w2], 16)
                        if final:
                            for n in range(2 * NBLK):
                                eng.wait_ge(s_xo, n + 1)
                                eng.dma_start(out.rearrange("(t p) d -> p t d", p=P)[:, 2 * n:2 * n + 2, :],
                                              xs[:, 2 * n:2 * n + 2, :]).then_inc(s_out, 16)
                            eng.wait_ge(s_out, 16 * 2 * NBLK)

            stage.end()

        def attention_stage(a, qd, kd, od, loads=()):
            stage = Stage()
            sem = stage.sem
            tag = a.name
            s_qk, s_v, s_ones = sem("qk_loaded" + tag), sem("values_ready" + tag), sem("ones_ready" + tag)
            s_a, s_max, s_m = sem("max_scores_ready" + tag), sem("max_bank_done" + tag), sem("max_parts" + tag)
            s_sc, s_ex, s_pv = sem("scores_ready" + tag), sem("exp_done" + tag), sem("pv_done" + tag)
            s_acc, s_ost = sem("accumulator_moved" + tag), sem("attended_stored" + tag)
            PV0 = 2
            MC = 6
            with ExitStack() as tmp:
                Q = sb("Q" + tag, [P, 2, HG, a.NQ], BF16, tmp)
                K = sb("K" + tag, [P, 2, HG, a.NK], BF16, tmp)
                V = sb("V" + tag, [P, a.KT, HG, 32], FP32, tmp)
                NE = 2 + a.KT % 2
                E = sb("E" + tag, [P, NE, HG, BLK], FP32, tmp)
                O = sb("O" + tag, [P, BLK], FP32, tmp)
                mx = sb("mx" + tag, [P, a.NI, a.NKB], FP32, tmp)
                nm = sb("nm" + tag, [P, a.NI], FP32, tmp)
                nr = sb("nr" + tag, [P, 2, a.NI], FP32, tmp)
                mp = sb("mp" + tag, [P, a.NI, KM], BF16, tmp)
                blk = tmp.enter_context(nc.Block())

                def ebuf(s):
                    return 2 if s == a.KT - 1 and a.KT % 2 else s % 2

                @blk.sync
                def _(eng):
                    def load(j, par):
                        for r in range(len(Q_PARTS)):
                            for buf, src, part in ((Q, qd, Q_PARTS[r]), (K, kd, K_PARTS[r])):
                                eng.dma_start(buf[DK * r:DK * (r + 1), par, :, :].rearrange("p a h t -> p (a h) t"),
                                              src[j, :, part, :].rearrange("a (h f) t -> f (a h) t", f=DK)).then_inc(s_qk, 16)

                    def loaded(j):
                        return 16 * 2 * len(Q_PARTS) * (j + 1)

                    def store(u, j, b):
                        eng.wait_ge(s_acc, u + 1)
                        eng.dma_start(od[j, :, ds(b * BLK, BLK)].rearrange("a p t -> p (a t)"), O[:, :]).then_inc(s_ost, 16)

                    load(ds(0, 1), ds(0, 1))
                    eng.wait_ge(s_qk, loaded(0))
                    load(ds(1, 1), ds(1, 1))
                    for dst, src, s in loads:
                        eng.dma_start(dst[:, :, :], chunked(src)).then_inc(ld[s], 16)
                    with eng.Fori(0, a.J - 2) as j:
                        for b in range(a.NB):
                            store(j * a.NB + b, ds(j, 1), b)
                        eng.wait_ge(s_qk, loaded(j + 1))
                        load(ds(j + 2, 1), ds(j % 2, 1))
                    with eng.Fori(a.J - 2, a.J) as j:
                        for b in range(a.NB):
                            store(j * a.NB + b, ds(j, 1), b)
                    eng.wait_ge(s_ost, 16 * a.U)

                @blk.gpsimd
                def _(eng):
                    stage.clear_before(eng)
                    eng.memset(V[:, :, :, DK:32], 1.0).then_inc(s_ones, 1)
                    eng.wait_ge(s_ones, 1)
                    eng.memset(K[KQ:KQ + KM, :, :, :], 1.0).then_inc(s_ones, 1)
                    eng.wait_ge(s_ones, 2)

                    def values(c, base):
                        k0, k1 = c * a.VC, min((c + 1) * a.VC, a.KT)
                        full = [k for k in range(k0, k1) if a.KW[k] == P]
                        for lo, n, wd in ((k0, len(full), P), (k0 + len(full), k1 - k0 - len(full), a.KW[-1])):
                            if n:
                                last = eng.tensor_copy(V[0:wd, lo:lo + n, :, 0:DK],
                                                       v_all[0:wd, ds(base + lo, n), :].rearrange("p k (h f) -> p k h f", h=HG))
                        last.then_inc(s_v, 1)

                    for c in range(a.NVC):
                        values(c, 0)
                    with eng.Fori(1, a.J) as j:
                        for c in range(a.NVC):
                            eng.wait_ge(s_pv, PV0 + (j * a.NB - 1) * a.KT + min((c + 1) * a.VC, a.KT))
                            values(c, j * a.KT)

                def find_max(eng, u, k):
                    i, kb = k // a.NKB, k % a.NKB
                    h, qt = i // TB, i % TB
                    j, b = u // a.NB, u % a.NB
                    return eng.matmul(ps[:, 5 + k % 3, 0:a.KBW[kb]],
                                      Q[0:KQ, ds(j % 2, 1), h, ds(b * BLK + qt * P, P)].rearrange("p a t -> p (a t)"),
                                      K[0:KQ, ds(j % 2, 1), h, kb * BLK:kb * BLK + a.KBW[kb]].rearrange("p a t -> p (a t)"),
                                      start=True, stop=True)

                @blk.tensor
                def _(eng):
                    def search(u, k, first=False):
                        if k >= 3:
                            eng.wait_ge(s_max, u * a.NA + k - 2)
                        elif k == 0 and not first:
                            eng.wait_ge(s_max, u * a.NA)
                        find_max(eng, u, k).then_inc(s_a, 1)

                    def lay_maxima(u, event):
                        eng.wait_ge(s_m, MC * (u + 1))
                        for p in range(2):
                            if event is not None:
                                eng.wait_ge(s_ex, event + p - 1)
                            for h in range(2):
                                for qt in range(TB):
                                    last = eng.matmul(ps[KQ:KQ + KM, 2 * p + h, qt * P:(qt + 1) * P],
                                                      mp[:, (2 * p + h) * TB + qt, :], identb[:, :], start=True, stop=True)
                            last.then_inc(s_sc, 1)

                    def scores(u, s, event):
                        j, b = u // a.NB, u % a.NB
                        for p in range(2):
                            eng.wait_ge(s_ex, event + p - 1)
                            for h in range(2 * p, 2 * p + 2):
                                last = eng.matmul(ps[0:a.KW[s], h, :],
                                                  K[0:KQ + KM, ds(j % 2, 1), h, s * P:s * P + a.KW[s]].rearrange("p a t -> p (a t)"),
                                                  Q[0:KQ + KM, ds(j % 2, 1), h, ds(b * BLK, BLK)].rearrange("p a t -> p (a t)"),
                                                  start=True, stop=True)
                            last.then_inc(s_sc, 1)

                    def weigh(u, s, event):
                        if s == 0:
                            eng.wait_ge(s_acc, u)
                        eng.wait_ge(s_ex, event + 2)
                        if s % a.VC == 0:
                            eng.wait_ge(s_v, (u // a.NB) * a.NVC + s // a.VC + 1)
                        for h in range(HG):
                            last = eng.matmul(ps[32 * h:32 * h + 32, 4, :], V[0:a.KW[s], s, h, :], E[0:a.KW[s], ebuf(s), h, :],
                                              start=(s == 0), stop=(s == a.KT - 1))
                        last.then_inc(s_pv, 1)

                    def unit(u, first_event, lookahead, first):
                        n, k = first_event, 0
                        before = None
                        for s in range(a.KT):
                            scores(u, s, n)
                            if before is not None:
                                weigh(u, *before) if not (first and before[0] == 0) else weigh_first(u, *before)
                            before = (s, n)
                            n += 2
                            if lookahead:
                                upto = a.NA * min(s + 1, a.A_STEPS) // a.A_STEPS
                                while k < upto:
                                    search(u + 1, k)
                                    k += 1
                                if s == a.M_STEP:
                                    lay_maxima(u + 1, n)
                                    n += 2
                        weigh(u, *before)

                    def weigh_first(u, s, event):
                        eng.wait_ge(s_ex, event + 2)
                        eng.wait_ge(s_v, 1)
                        for h in range(HG):
                            last = eng.matmul(ps[32 * h:32 * h + 32, 4, :], V[0:a.KW[s], s, h, :], E[0:a.KW[s], ebuf(s), h, :],
                                              start=True, stop=False)
                        last.then_inc(s_pv, 1)

                    eng.sem_inc(s_pv, PV0)
                    eng.wait_ge(s_ones, 2)
                    eng.wait_ge(s_qk, 16 * 2 * len(Q_PARTS))
                    for k in range(a.NA):
                        search(0, k, first=True)
                    lay_maxima(0, None)
                    if a.NB == 1:
                        eng.wait_ge(s_qk, 2 * 16 * 2 * len(Q_PARTS))
                    unit(0, 2, True, True)
                    with eng.Fori(1, a.U - 1) as u:
                        eng.wait_ge(s_qk, 16 * 2 * len(Q_PARTS) * ((u + 1) // a.NB + 1))
                        unit(u, u * a.EV + 2, True, False)
                    unit(a.U - 1, (a.U - 1) * a.EV + 2, False, False)

                @blk.scalar
                def _(eng):
                    def expose(u, s, event):
                        for p in range(2):
                            eng.wait_ge(s_sc, event + p + 1)
                            if p == 0:
                                eng.wait_ge(s_pv, PV0 + u * a.KT + s - 1)
                            eng.activation(E[0:a.KW[s], ebuf(s), 2 * p:2 * p + 2, :], ps[0:a.KW[s], 2 * p:2 * p + 2, :],
                                           ACT.Exp, scale=SCALE).then_inc(s_ex, 1)

                    def place_maxima(u, event):
                        j, b = u // a.NB, u % a.NB
                        for p in range(2):
                            eng.wait_ge(s_sc, event + p + 1)
                            eng.activation(Q[KQ:KQ + KM, ds(j % 2, 1), 2 * p:2 * p + 2, ds(b * BLK, BLK)].rearrange("p a h t -> p (a h) t"),
                                           ps[KQ:KQ + KM, 2 * p:2 * p + 2, :], ACT.Copy).then_inc(s_ex, 1)

                    def unit(u, first_event, lookahead):
                        n = first_event
                        for s in range(a.KT):
                            expose(u, s, n)
                            n += 2
                            if lookahead and s == a.M_STEP:
                                place_maxima(u + 1, n)
                                n += 2

                    place_maxima(0, 0)
                    with eng.Fori(0, a.U - 1) as u:
                        unit(u, u * a.EV + 2, True)
                    unit(a.U - 1, (a.U - 1) * a.EV + 2, False)

                @blk.vector
                def _(eng):
                    def reduce(u, k):
                        i, kb = k // a.NKB, k % a.NKB
                        eng.wait_ge(s_a, u * a.NA + k + 1)
                        eng.tensor_reduce(mx[:, i, kb:kb + 1], ps[:, 5 + k % 3, 0:a.KBW[kb]], AX.X, ALU.max).then_inc(s_max, 1)

                    def maxima(u):
                        for k in range(a.NA):
                            reduce(u, k)
                        m = u * MC
                        eng.wait_ge(s_max, (u + 1) * a.NA)
                        eng.tensor_reduce(nm[:, :], mx[:, :, :], AX.X, ALU.max, negate=True).then_inc(s_m, 1)
                        eng.wait_ge(s_m, m + 1)
                        eng.tensor_copy(mp[:, :, 0], nm[:, :]).then_inc(s_m, 1)
                        eng.wait_ge(s_m, m + 2)
                        eng.tensor_tensor(nr[:, 0, :], nm[:, :], mp[:, :, 0], ALU.subtract).then_inc(s_m, 1)
                        eng.wait_ge(s_m, m + 3)
                        eng.tensor_copy(mp[:, :, 1], nr[:, 0, :]).then_inc(s_m, 1)
                        eng.wait_ge(s_m, m + 4)
                        eng.tensor_tensor(nr[:, 1, :], nr[:, 0, :], mp[:, :, 1], ALU.subtract).then_inc(s_m, 1)
                        eng.wait_ge(s_m, m + 5)
                        eng.tensor_copy(mp[:, :, 2], nr[:, 1, :]).then_inc(s_m, 1)

                    def move_out(u, first=False):
                        eng.wait_ge(s_pv, PV0 + (u + 1) * a.KT)
                        if not first:
                            eng.wait_ge(s_ost, 16 * u)
                        eng.tensor_copy(O[:, :], ps[:, 4, :]).then_inc(s_acc, 1)

                    maxima(0)
                    maxima(1)
                    move_out(0, True)
                    with eng.Fori(1, a.U - 1) as u:
                        maxima(u + 1)
                        move_out(u)
                    move_out(a.U - 1)

            stage.end()

        def out_stage(a, od, rd, wt, wload, bias, gk, into=xs):
            stage = Stage()
            sem = stage.sem
            tag = "o" + a.name
            s_s, s_r, s_rs, s_o, s_rb = (sem(n + tag) for n in
                                         ("sums_loaded", "inverse_done", "inverse_stored", "attended_loaded", "inverse_loaded"))
            s_n, s_y, s_g, s_x, s_b = (sem(n + tag) for n in ("divided", "projected", "gated", "residual_done", "bias_added"))
            HPB = P // a.J
            TPP = HG * a.NQ // HPB
            with ExitStack() as tmp:
                R = sb("R" + tag, [P, KC, S], FP32, tmp)
                sums = sb("sums" + tag, [P, TPP], FP32, tmp)
                inv = sb("inv" + tag, [P, TPP], FP32, tmp)
                y = sb("y" + tag, [P, 2, 2, D], FP32, tmp)
                blk = tmp.enter_context(nc.Block())

                def halves(buf, j):
                    g, half = j % G, j // G
                    return buf[GW * (g % 2):GW * (g % 2) + GW, g // 2, half * a.NQ:(half + 1) * a.NQ]

                @blk.sync
                def _(eng):
                    for j in range(a.J):
                        eng.dma_start(sums[HPB * j:HPB * (j + 1), :],
                                      od[j].rearrange("(h r) t -> h r t", r=32)[:, DK, :]
                                      .rearrange("h (s t) -> h s t", t=TPP)).then_inc(s_s, 16)
                    eng.wait_ge(s_r, 1)
                    eng.dma_start(rd.rearrange("j h (s t) -> (j h s) t", t=TPP), inv[:, :]).then_inc(s_rs, 16)
                    eng.wait_ge(s_rs, 16)
                    for j in range(a.J):
                        dst = halves(R, j)
                        for h in range(HG):
                            eng.dma_start(dst[DK * h:DK * (h + 1), :],
                                          rd[j, h, :].partition_broadcast(DK)).then_inc(s_rb, 16)

                @blk.scalar
                def _(eng):
                    for j in range(a.J):
                        eng.dma_start(halves(hT, j), od[j].rearrange("(h r) t -> h r t", r=32)[:, 0:DK, :]).then_inc(s_o, 16)

                @blk.gpsimd
                def _(eng):
                    stage.clear_before(eng)
                    for half in range(2):
                        t0, t1 = half * T // 2, (half + 1) * T // 2
                        ins = eng.tensor_tensor(into[:, t0:t1, :], xs[:, t0:t1, :], bias(half).to_broadcast([P, T // 2, D]), ALU.add)
                    ins.then_inc(s_b, 1)

                @blk.vector
                def _(eng):
                    eng.wait_ge(s_s, 16 * a.J)
                    eng.reciprocal(inv[:, :], sums[:, :]).then_inc(s_r, 1)
                    eng.wait_ge(s_o, 16 * a.J)
                    eng.wait_ge(s_rb, 16 * a.J * HG)
                    for b in range(NBLK):
                        v = hT[:, :, b * BLK:(b + 1) * BLK]
                        eng.tensor_tensor(v, v, R[:, :, b * BLK:(b + 1) * BLK], ALU.mult).then_inc(s_n, 1)
                    eng.wait_ge(s_b, 1)
                    for n in range(T // 2):
                        v = into[:, 2 * n:2 * n + 2, :]
                        eng.wait_ge(s_y, n + 1)
                        p = ps[:, n % 4, :].rearrange("p (t d) -> p t d", t=2)
                        if gk is None:
                            eng.tensor_tensor(v, p, v, ALU.add).then_inc(s_x, 1)
                        else:
                            g = gate[:, n // (T // 4), gk:gk + 1, :].to_broadcast([P, 2, D])
                            if n >= 2:
                                eng.wait_ge(s_x, n - 1)
                            eng.tensor_tensor(y[:, n % 2, :, :], p, g, ALU.mult).then_inc(s_g, 1)
                            eng.wait_ge(s_g, n + 1)
                            eng.tensor_tensor(v, v, y[:, n % 2, :, :], ALU.add).then_inc(s_x, 1)

                @blk.tensor
                def _(eng):
                    eng.wait_ge(ld[wload], 16)
                    for n in range(T // 2):
                        eng.wait_ge(s_n, n // 2 + 1)
                        if n >= 4:
                            eng.wait_ge(s_x if gk is None else s_g, n - 3)
                        for t in range(2):
                            for kc in range(KC):
                                last = eng.matmul(ps[:, n % 4, t * D:(t + 1) * D], hT[:, kc, (2 * n + t) * P:(2 * n + t + 1) * P],
                                                  wt[:, kc, :], start=(kc == 0), stop=(kc == KC - 1))
                        last.then_inc(s_y, 1)

            stage.end()

        def part_rows(dst, a, c, t0):
            half = t0 // a.NQ if a.J > G else 0
            j = half * G + c * (P // GW)
            return dst[j:j + P // GW].rearrange("j f r t -> (j f) r t"), t0 - half * (S // 2 if a.J > G else 0)

        def v_place(a, tt, swap):
            if a.J == G:
                return lambda v, nt: v[0:nt, 0:a.J * a.KT, :].rearrange("p (g k) f -> p g k f", g=G)[:, :, tt, :]
            half = tt // a.KT ^ swap
            return lambda v, nt: v[0:nt, half * G * a.KT:(half + 1) * G * a.KT, :]\
                .rearrange("p (g k) f -> p g k f", g=G)[:, :, tt % a.KT, :]

        def projections(a, n, wt, wload, qcol, vrow, swap=0):
            jobs = []
            for b in range(NBLK):
                for which, dst in ((0, q_dram[n]), (1, k_dram[n])):
                    for c in range(KC):
                        rows_, t0 = part_rows(dst, a, c, b * BLK)
                        if which and swap:
                            rows_, _ = part_rows(dst, a, c, (b * BLK + S // 2) % S)
                        o = which * D + c * P
                        jobs.append(("qk", hT, ((lambda kc, o=o: wt[:, kc, o:o + P]), wload),
                                     qcol + which * KC + c, rows_, (b * BLK, t0), BLK, b))
                for t in range(TB):
                    jobs.append(("v", hT, ((lambda kc: wt[:, kc, 2 * D:3 * D]), wload), vrow, b * TB + t, P,
                                 v_place(a, b * TB + t, swap), b))
            return jobs

        def cross_projections():
            a, jobs = attn[1], []
            wload = (("wcq", 48), ("ctx", 16))
            for b in range((SC + BLK - 1) // BLK):
                nt = min(BLK, SC - b * BLK)
                for c in range(KC):
                    rows_, _ = part_rows(k_dram[1], a, c, 0)
                    o = D + c * P
                    jobs.append(("qk", cT, ((lambda kc, o=o: wcq[:, kc, o:o + P]), wload), COL["ck_b"] + c, rows_,
                                 (b * BLK, b * BLK), nt, None))
                for tt in range(b * TB, min((b + 1) * TB, a.KT)):
                    jobs.append(("v", cT, ((lambda kc: wcq[:, kc, 2 * D:3 * D]), wload), ROW["cv_b"], tt, a.KW[tt],
                                 v_place(a, tt, 0), None))
            for b in range(NBLK):
                for c in range(KC):
                    rows_, _ = part_rows(q_dram[1], a, c, 0)
                    jobs.append(("qk", hT, ((lambda kc, o=c * P: wcq[:, kc, o:o + P]), wload), COL["cq_b"] + c, rows_,
                                 (b * BLK, b * BLK), BLK, b))
            return jobs

        def col(name):
            return lambda kc, half: cols[:, COL[name] + kc:COL[name] + kc + 1]

        def modulation(k):
            return (lambda kc, half: shift[:, 2 * (2 * k + 1) + kc, half:half + 1],
                    lambda kc, half: shift[:, 2 * (2 * k) + kc, half:half + 1])

        norm_stage("n1", 0, col("ln1_g"), col("ln1_b"),
                   lambda: projections(attn[0], 0, wq, (("wq", 16),), COL["in_b"], ROW["v_b"]))
        attention_stage(attn[0], q_dram[0], k_dram[0], o_dram[0])
        out_stage(attn[0], o_dram[0], r_dram[0], wo, "wo", lambda half: rows[:, ROW["out_b"]:ROW["out_b"] + 1, :], None)
        norm_stage("n2", 0, col("ln2_g"), col("ln2_b"), cross_projections)
        attention_stage(attn[1], q_dram[1], k_dram[1], o_dram[1],
                        ((wq, w["qkv2"], "wq2"), (wo, w["proj2"], "wo2"), (wcq, w["cqkv2"], "wcq2")))
        out_stage(attn[1], o_dram[1], r_dram[1], wco, "wco", lambda half: rows[:, ROW["co_b"]:ROW["co_b"] + 1, :], None)
        norm_stage("n3", 0, col("ln3_g"), col("ln3_b"), None, (COL["ff1_b"], ACT.Gelu, False, (w["ff1"], w["ff2"]), ("wf1", "wf2"), False))

        norm_stage("n4", 1, *modulation(0),
                   lambda: projections(attn[2], 2, wq, (("wq2", 16),), COL["qkv2_b"], ROW["v2_b"]))
        attention_stage(attn[2], q_dram[2], k_dram[2], o_dram[2], ((wco, w["cproj2"], "wco2"),))
        out_stage(attn[2], o_dram[2], r_dram[2], wo, "wo2", lambda half: gbias[:, half, 0:1, :], 0, xmid)
        norm_stage("n5", 1, *modulation(1),
                   lambda: projections(attn[3], 3, wcq, (("wcq2", 16),), COL["cqkv2_b"], ROW["cv2_b"], 1), src=xmid)
        attention_stage(attn[3], q_dram[3], k_dram[3], o_dram[3])
        out_stage(attn[3], o_dram[3], r_dram[3], wco, "wco2", lambda half: gbias[:, half, 1:2, :], 1)
        norm_stage("n6", 1, *modulation(2), None,
                   (COL["fc1_b"], ACT.Gelu_apprx_tanh, True, (w["fc12"], w["fc22"]), ("wf12", "wf22"), True))


def kernel(**inputs):
    import numpy as np
    import concourse.bacc as bacc
    from concourse.bass_utils import run_bass_kernel_spmd

    a = {k: np.asarray(v) for k, v in inputs.items()}
    L0, L1 = "L0_xattn_", "L1_xattn_"

    def t(name):
        return np.ascontiguousarray(a[name].T)

    col_at, cols = {}, []
    for name, v in (("ln1_g", a[L0 + "ln1_g"]), ("ln1_b", a[L0 + "ln1_b"]), ("ln2_g", a[L0 + "ln2_g"]),
                    ("ln2_b", a[L0 + "ln2_b"]), ("ln3_g", a[L0 + "ln3_g"]), ("ln3_b", a[L0 + "ln3_b"]),
                    ("in_b", a[L0 + "in_proj_b"]), ("cq_b", a[L0 + "cq_b"]), ("ck_b", a[L0 + "ck_b"]),
                    ("ff1_b", a[L0 + "ff1_b"]), ("qkv2_b", a[L1 + "attn_qkv_b"]), ("cqkv2_b", a[L1 + "crs_qkv_b"]),
                    ("fc1_b", a[L1 + "mlp_fc1_b"]), ("ada_b", a[L1 + "ada_b"])):
        col_at[name] = len(cols)
        cols += list(v.reshape(-1, 128))
    row_at, rows = {}, []
    for name, vs in (("v_b", [a[L0 + "in_proj_b"][512:]]), ("out_b", [a[L0 + "out_proj_b"]]), ("cv_b", [a[L0 + "cv_b"]]),
                     ("co_b", [a[L0 + "co_b"]]), ("ff2_b", [a[L0 + "ff2_b"]]), ("v2_b", [a[L1 + "attn_qkv_b"][512:]]),
                     ("cv2_b", [a[L1 + "crs_qkv_b"][512:]]),
                     ("gate", [a[L1 + "ada_b"][k * 256:(k + 1) * 256] for k in (2, 5, 8)]),
                     ("out2", [a[L1 + "attn_proj_b"], a[L1 + "crs_proj_b"], a[L1 + "mlp_fc2_b"]])):
        row_at[name] = len(rows)
        rows += vs
    arrays = {
        "x": a["x"].reshape(2048, 256), "ctxT": np.ascontiguousarray(a["ctx_1024"][0].T),
        "cols": np.ascontiguousarray(np.stack(cols, 1)), "rows": np.ascontiguousarray(np.stack(rows, 0)),
        "in_proj": t(L0 + "in_proj_w"), "out_proj": t(L0 + "out_proj_w"), "cq": t(L0 + "cq_w"), "ck": t(L0 + "ck_w"),
        "cv": t(L0 + "cv_w"), "co": t(L0 + "co_w"), "ff1": t(L0 + "ff1_w"), "ff2": t(L0 + "ff2_w"),
        "qkv2": a[L1 + "attn_qkv_w"], "proj2": a[L1 + "attn_proj_w"], "cqkv2": a[L1 + "crs_qkv_w"],
        "cproj2": a[L1 + "crs_proj_w"], "fc12": a[L1 + "mlp_fc1_w"], "fc22": a[L1 + "mlp_fc2_w"], "ada": a[L1 + "ada_w"],
    }
    nc = bacc.Bacc("TRN2", target_bir_lowering=False, num_devices=1)
    feeds, w = {}, {}
    for name, v in arrays.items():
        feeds["in_" + name] = np.ascontiguousarray(v)
        w[name] = nc.dram_tensor("in_" + name, v.shape, mybir.dt.from_np(v.dtype), kind="ExternalInput").ap()
    out = nc.dram_tensor("out_0", (2048, 256), FP32, kind="ExternalOutput").ap()
    w["col_at"], w["row_at"] = col_at, row_at
    build(nc, w["x"], w["ctxT"], w, out)
    r = run_bass_kernel_spmd(nc, [feeds], core_ids=[0])
    return r.results[0]["out_0"].reshape(1, 2048, 256)
```

```python
import concourse.bass as bass
from concourse import mybir
from contextlib import ExitStack

FP32 = mybir.dt.float32
BF16 = mybir.dt.bfloat16
ALU = mybir.AluOpType
ACT = mybir.ActivationFunctionType
AX = mybir.AxisListType
ds = bass.ds

P = 128
S = 2048
D = 256
KC = D // P
T = S // P
BLK = 512
NBLK = S // BLK
TB = BLK // P
SC = 1601
H = 16
DK = D // H
HG = 4
G = H // HG
GW = HG * DK
F = 1024
FC = F // P
SCALE = 0.25

Q_PARTS = (0, 0, 0, 1, 1, 2)
K_PARTS = (0, 1, 2, 0, 1, 0)
KQ = len(Q_PARTS) * DK
KM = 3


class Attention:

    def __init__(self, name, stages, queries, keys):
        self.name = name
        self.J = stages
        self.NQ = queries
        self.NK = keys
        self.NB = queries // BLK
        self.U = stages * self.NB
        self.KT = (keys + P - 1) // P
        self.KW = [min(P, keys - P * k) for k in range(self.KT)]
        self.NKB = (keys + BLK - 1) // BLK
        self.KBW = [min(BLK, keys - BLK * k) for k in range(self.NKB)]
        self.NI = HG * TB
        self.NA = self.NI * self.NKB
        self.EV = 2 * (self.KT + 1)
        self.M_STEP = self.KT - 1
        self.AHEAD = 3
        self.L = self.NA * self.AHEAD // self.KT
        self.VC = 4
        self.NVC = (self.KT + self.VC - 1) // self.VC


def build(nc, x, ctxT, w, out):
    ctx = ExitStack()
    with ctx:
        def sb(name, shape, dt=FP32, stack=ctx):
            return stack.enter_context(nc.sbuf_tensor(name, shape, dt))

        def lasting_sem(name):
            return ctx.enter_context(nc.semaphore(name))

        class Stage:
            last = None

            def __init__(self):
                self.stack = ExitStack()
                self.sems = []
                self.before = Stage.last
                Stage.last = self

            def sem(self, name):
                self.sems.append(self.stack.enter_context(nc.semaphore(name)))
                return self.sems[-1]

            def clear_before(self, pool):
                for s in self.before.sems if self.before else ():
                    pool.sem_clear(s)

            def end(self):
                if self.before:
                    self.before.stack.close()

        def dram(name, shape, dt=FP32):
            return nc.dram_tensor(name, shape, dt, kind="Internal").ap()

        xs = sb("xs", [P, T, D])
        hT = sb("hT", [P, KC, S])
        cT = sb("cT", [P, KC, SC])
        v_all = sb("v_all", [P, 64, GW])
        ident = sb("ident", [P, P])
        identb = sb("identb", [P, P], BF16)
        wq = sb("wq", [P, KC, 3 * D])
        wo = sb("wo", [P, KC, D])
        wcq = sb("wcq", [P, KC, 3 * D])
        wco = sb("wco", [P, KC, D])
        cols = sb("cols", [P, w["cols"].shape[1]])
        rows = sb("rows", [P, w["rows"].shape[0], D])
        shift = sb("shift", [P, 12, 2])
        gate = sb("gate", [P, 2, 3, D])
        gbias = sb("gbias", [P, 2, 3, D])
        eps = sb("eps", [P, 2])
        ps = ctx.enter_context(nc.psum_tensor("ps", [P, 8, BLK], FP32))

        COL = w["col_at"]
        ROW = w["row_at"]

        attn = [Attention("a0", G, S, S), Attention("a1", G, S, SC),
                Attention("a2", 2 * G, S // 2, S // 2), Attention("a3", 2 * G, S // 2, S // 2)]
        q_dram = [dram(f"q_parts{a.name}", [a.J, GW, 3, a.NQ], BF16) for a in attn]
        k_dram = [dram(f"k_parts{a.name}", [a.J, GW, 3, a.NK], BF16) for a in attn]

        ld = {n: lasting_sem("ld_" + n) for n in ("x", "ctx", "small", "wq", "wo", "wcq", "wco", "wf1", "wf2", "ada",
                                          "wq2", "wo2", "wcq2", "wco2", "wf12", "wf22")}
        s_id = lasting_sem("identities_made")

        def chunked(ap):
            return ap.rearrange("(c p) n -> p c n", p=P)

        stage = Stage()
        sem = stage.sem
        s_silu, s_modp, s_mod, s_gatep, s_gate = (sem(n) for n in ("silu_done", "mod_ready", "mod_done", "gate_ready", "gate_done"))
        with ExitStack() as tmp:
            ada = sb("ada", [P, KC, 9 * D], FP32, tmp)
            sil = sb("sil", [P, KC, 2], FP32, tmp)
            silr = sb("silr", [P, KC, 2, P], FP32, tmp)
            zero = sb("zero", [P, P], FP32, tmp)
            blk = tmp.enter_context(nc.Block())
            VECS = (0, 1, 3, 4, 6, 7)
            GATES = (2, 5, 8)

            @blk.sync
            def _(eng):
                eng.dma_start(cT[:, :, :], chunked(ctxT)).then_inc(ld["ctx"], 16)
                eng.dma_start(cols[:, :], w["cols"]).then_inc(ld["small"], 16)
                eng.dma_start(rows[:, :, :], w["rows"].partition_broadcast(P)).then_inc(ld["small"], 16)
                eng.dma_start(xs[:, :, :], x.rearrange("(t p) d -> p t d", p=P)).then_inc(ld["x"], 16)
                eng.dma_start(wq[:, :, :], chunked(w["in_proj"])).then_inc(ld["wq"], 16)
                eng.dma_start(wo[:, :, :], chunked(w["out_proj"])).then_inc(ld["wo"], 16)
                for i, n in enumerate(("cq", "ck", "cv")):
                    eng.dma_start(wcq[:, :, i * D:(i + 1) * D], chunked(w[n])).then_inc(ld["wcq"], 16)
                eng.dma_start(wco[:, :, :], chunked(w["co"])).then_inc(ld["wco"], 16)

            @blk.gpsimd
            def _(eng):
                stage.clear_before(eng)
                eng.memset(ident[:, :], 0.0).then_inc(s_id, 1)
                eng.memset(identb[:, :], 0.0).then_inc(s_id, 1)
                eng.memset(zero[:, :], 0.0).then_inc(s_id, 1)
                eng.memset(eps[:, 0:1], 1e-5).then_inc(s_id, 1)
                eng.memset(eps[:, 1:2], 1e-6).then_inc(s_id, 1)
                eng.wait_ge(s_id, 2)
                for m in (ident, identb):
                    eng.affine_select(out=m[:, :], in_=m[:, :], compare_op=ALU.not_equal, fill=1.0,
                                      base=0, pattern=[[-1, P]], channel_multiplier=1).then_inc(s_id, 1)

            @blk.scalar
            def _(eng):
                eng.dma_start(ada[:, :, :], chunked(w["ada"])).then_inc(ld["ada"], 16)
                eng.wait_ge(ld["ctx"], 16)
                eng.activation(sil[:, :, :], cT[:, :, 0:2], ACT.Silu).then_inc(s_silu, 1)
                eng.wait_ge(s_silu, 1)
                eng.wait_ge(s_id, 3)
                for kc in range(KC):
                    for half in range(2):
                        eng.activation(silr[:, kc, half, :], zero[:, :], ACT.Identity,
                                       bias=sil[:, kc, half:half + 1]).then_inc(s_silu, 1)

            @blk.tensor
            def _(eng):
                eng.wait_ge(ld["ada"], 16)
                eng.wait_ge(s_silu, 1)
                for i, v in enumerate(VECS):
                    for c in range(KC):
                        for kc in range(KC):
                            last = eng.matmul(ps[:, 0, 4 * i + 2 * c:4 * i + 2 * c + 2],
                                              ada[:, kc, v * D + c * P:v * D + (c + 1) * P], sil[:, kc, :],
                                              start=(kc == 0), stop=(kc == KC - 1))
                last.then_inc(s_modp, 1)
                eng.wait_ge(s_silu, 1 + 2 * KC)
                for half in range(2):
                    for k, v in enumerate(GATES):
                        for kc in range(KC):
                            last = eng.matmul(ps[:, 1 + half * 3 + k, 0:D], silr[:, kc, half, :],
                                              ada[:, kc, v * D:(v + 1) * D], start=(kc == 0), stop=(kc == KC - 1))
                last.then_inc(s_gatep, 1)

            @blk.vector
            def _(eng):
                eng.wait_ge(ld["small"], 32)
                eng.wait_ge(s_modp, 1)
                for i, v in enumerate(VECS):
                    for c in range(KC):
                        n = 2 * i + c
                        b = COL["ada_b"] + 2 * v + c
                        eng.tensor_scalar(shift[:, n, :], ps[:, 0, 2 * n:2 * n + 2], cols[:, b:b + 1], float(i % 2),
                                          ALU.add, ALU.add).then_inc(s_mod, 1)
                eng.wait_ge(s_gatep, 1)
                for half in range(2):
                    for k in range(3):
                        eng.tensor_tensor(gate[:, half, k, :], ps[:, 1 + half * 3 + k, 0:D],
                                          rows[:, ROW["gate"] + k, :], ALU.add).then_inc(s_gate, 1)
                eng.wait_ge(s_gate, 6)
                for half in range(2):
                    for k in range(3):
                        eng.tensor_tensor(gbias[:, half, k, :], gate[:, half, k, :],
                                          rows[:, ROW["out2"] + k, :], ALU.mult).then_inc(s_gate, 1)

        stage.end()

        def dense_stage(tag, e, scale_at, shift_at, projected=None, mlp=None, attended=None, mid=False):
            stage = Stage()
            sem = stage.sem
            s_stat, s_var, s_std, s_rstd = (sem(n + tag) for n in ("bn_stats_done", "variance_done", "std_done", "rstd_done"))
            s_h, s_tp, s_ev = (sem(n + tag) for n in ("normed_ready", "transposed_ready", "transposed_moved"))
            s_pj, s_pjfree = sem("projected_ready" + tag), sem("projection_bank_free" + tag)
            s_y, s_yfree, s_g, s_x, s_b = (sem(n + tag) for n in ("token_major_ready", "token_major_bank_free", "gated",
                                                                  "residual_done", "bias_added"))
            OUT = attended is not None
            TU = 2 if OUT else 1
            with ExitStack() as tmp:
                st = sb("st" + tag, [P, T, 6], FP32, tmp)
                mv = sb("mv" + tag, [P, T, 2], FP32, tmp)
                std = sb("std" + tag, [P, T], FP32, tmp)
                rstd = sb("rstd" + tag, [P, T], FP32, tmp)
                h = sb("h" + tag, [P, T, D], FP32, tmp)
                gated_y = sb("gated_y" + tag, [P, 2, 2, D], FP32, tmp)
                src = xs
                if OUT:
                    wt, wload, bias, gk = attended
                    otok = hT[:, :, :].rearrange("p c (t n) -> p (c t) n", n=D)
                    oT = sb("oT" + tag, [P, 2, KC, BLK], FP32, tmp)
                    aT = sb("aT" + tag, [P, KC, S], FP32, tmp)
                    if mid:
                        src = sb("xmid" + tag, [P, T, D], FP32, tmp)
                else:
                    aT = hT
                NPART = 4
                if projected is not None:
                    jobs_of = projected(aT)
                    jobs = [(i, job) for i in sorted(jobs_of) for job in jobs_of[i]]
                    parts = sb("parts" + tag, [P, NPART, 3, BLK], BF16, tmp)
                    rest = sb("rest" + tag, [P, NPART, BLK], FP32, tmp)
                    s_q1, s_q2, s_q3 = (sem(n + tag) for n in ("part1_done", "part2_done", "part3_done"))
                    s_stored = [sem(f"parts_stored{i}" + tag) for i in range(NPART)]
                else:
                    fcol, func, mgate, (w1, w2), (s_w1, s_w2), final = mlp
                    wf1 = sb("wf1" + tag, [P, KC, F], FP32, tmp)
                    wf2 = sb("wf2" + tag, [P, FC, D], FP32, tmp)
                    hid = sb("hid" + tag, [P, FC, BLK], FP32, tmp)
                    s_hid, s_xb, s_out = (sem(n + tag) for n in ("hidden_ready", "mlp_bias_added", "stored"))
                blk = tmp.enter_context(nc.Block())

                ROUNDS = range(0 if OUT else 1, NBLK + 3)

                def here(b):
                    return 0 <= b < NBLK

                def t_event(b, normed, kc):
                    n = 0
                    for i in ROUNDS:
                        for blk_, nrm in ((i, False), (i - 2, True)):
                            if here(blk_) and (nrm or OUT):
                                if (blk_, nrm) == (b, normed):
                                    return n + kc
                                n += KC

                def y_event(b, hidden, j):
                    n = 0
                    for i in ROUNDS:
                        for blk_, hid_ in ((i - 1, False), (i - 3, True)):
                            if here(blk_) and (OUT if not hid_ else mlp is not None):
                                if (blk_, hid_) == (b, hidden):
                                    return n + j
                                n += 2

                def transposes(eng, b, normed):
                    for kc in range(KC):
                        n = t_event(b, normed, kc)
                        if n >= 3:
                            eng.wait_ge(s_ev, n - 2)
                        for t in range(TB):
                            if normed and kc == 0:
                                eng.wait_ge(s_h, b * TB + t + 1)
                            source = h if normed else otok
                            last = eng.transpose(ps[:, n % 3, t * P:(t + 1) * P],
                                                 source[:, b * TB + t, kc * P:(kc + 1) * P], ident[:, :])
                        last.then_inc(s_tp, 1)

                def token_major(eng, b, j, n, terms):
                    if n >= 2:
                        eng.wait_ge(s_yfree, n - 1)
                    for t in range(2):
                        ts = terms(2 * j + t)
                        for i, (lhsT, rhs) in enumerate(ts):
                            last = eng.matmul(ps[:, 3 + n % 2, t * D:(t + 1) * D], lhsT, rhs,
                                              start=(i == 0), stop=(i == len(ts) - 1))
                    last.then_inc(s_y, 1)

                def project_heads(eng, b):
                    eng.wait_ge(s_ev, t_event(b, False, KC - 1) + 1)
                    for j in range(2):
                        token_major(eng, b, j, y_event(b, False, j),
                                    lambda t: [(oT[:, b % 2, kc, t * P:(t + 1) * P], wt[:, kc, :]) for kc in range(KC)])

                def bank(n):
                    return 5 + n % 3

                @blk.tensor
                def _(eng):
                    eng.wait_ge(s_id, 7)
                    waited = set()
                    if OUT:
                        eng.wait_ge(ld[wload], 16)
                    if mlp is not None:
                        eng.wait_ge(ld[s_w1], 16)
                        eng.wait_ge(ld[s_w2], 16)
                    n = 0
                    for i in range(0, NBLK + 3):
                        if OUT and here(i):
                            transposes(eng, i, False)
                        if OUT and here(i - 1):
                            project_heads(eng, i - 1)
                        if here(i - 2):
                            transposes(eng, i - 2, True)
                        b = i - 3
                        if here(b):
                            eng.wait_ge(s_ev, t_event(b, True, KC - 1) + 1)
                        if projected is not None:
                            for job in jobs_of.get(i, ()):
                                for name, value in job[2][1]:
                                    if name not in waited:
                                        waited.add(name)
                                        eng.wait_ge(ld[name], value)
                                if n >= 3:
                                    eng.wait_ge(s_pjfree, n - 2)
                                wj = job[2][0]
                                for kc in range(KC):
                                    if job[0] == "qk":
                                        last = eng.matmul(ps[:, bank(n), 0:job[6]], wj(kc),
                                                          job[1][:, kc, job[5][0]:job[5][0] + job[6]],
                                                          start=(kc == 0), stop=(kc == KC - 1))
                                    else:
                                        t0 = job[4] * P
                                        last = eng.matmul(ps[0:job[5], bank(n), 0:D], job[1][:, kc, t0:t0 + job[5]], wj(kc),
                                                          start=(kc == 0), stop=(kc == KC - 1))
                                last.then_inc(s_pj, 1)
                                n += 1
                        elif here(b):
                            for f in range(FC):
                                if n >= 3:
                                    eng.wait_ge(s_hid, n - 2)
                                for kc in range(KC):
                                    last = eng.matmul(ps[:, bank(n), :], wf1[:, kc, f * P:(f + 1) * P],
                                                      aT[:, kc, b * BLK:(b + 1) * BLK], start=(kc == 0), stop=(kc == KC - 1))
                                last.then_inc(s_pj, 1)
                                n += 1
                            eng.wait_ge(s_hid, n)
                            for j in range(2):
                                token_major(eng, b, j, y_event(b, True, j),
                                            lambda t: [(hid[:, f, t * P:(t + 1) * P], wf2[:, f, :]) for f in range(FC)])

                def move_transposed(eng, b, normed):
                    half = b // (NBLK // 2)
                    for kc in range(KC):
                        n = t_event(b, normed, kc)
                        eng.wait_ge(s_tp, n + 1)
                        if normed:
                            eng.activation(aT[:, kc, b * BLK:(b + 1) * BLK], ps[:, n % 3, :], ACT.Identity,
                                           bias=shift_at(kc, half), scale=scale_at(kc, half)).then_inc(s_ev, 1)
                        else:
                            if b >= 2 and kc == 0:
                                eng.wait_ge(s_y, y_event(b - 2, False, 1) + 1)
                            eng.activation(oT[:, b % 2, kc, :], ps[:, n % 3, :], ACT.Copy).then_inc(s_ev, 1)

                @blk.scalar
                def _(eng):
                    eng.wait_ge(ld["small"], 32)
                    eng.wait_ge(s_id, 7)
                    n = i_qk = 0
                    for i in range(0, NBLK + 3):
                        if OUT and here(i):
                            move_transposed(eng, i, False)
                        if here(i - 1):
                            a, z = (i - 1) * TB, i * TB
                            eng.wait_ge(s_var, z)
                            eng.activation(std[:, a:z], mv[:, a:z, 1], ACT.Sqrt, bias=eps[:, e:e + 1]).then_inc(s_std, 1)
                        if here(i - 2):
                            move_transposed(eng, i - 2, True)
                        if projected is not None:
                            for job in jobs_of.get(i, ()):
                                if job[0] == "qk":
                                    _, _, _, col, _, _, nt = job
                                    buf = i_qk % NPART
                                    if i_qk >= NPART:
                                        eng.wait_ge(s_stored[buf], 16 * (i_qk // NPART))
                                    eng.wait_ge(s_pj, n + 1)
                                    eng.activation(parts[:, buf, 0, 0:nt], ps[:, bank(n), 0:nt], ACT.Identity,
                                                   bias=cols[:, col:col + 1]).then_inc(s_q1, 1)
                                    i_qk += 1
                                n += 1
                        elif here(i - 3):
                            b = i - 3
                            for f in range(FC):
                                if f == 0 and b >= 1:
                                    eng.wait_ge(s_y, y_event(b - 1, True, 1) + 1)
                                eng.wait_ge(s_pj, n + 1)
                                eng.activation(hid[:, f, :], ps[:, bank(n), :], func,
                                               bias=cols[:, fcol + f:fcol + f + 1]).then_inc(s_hid, 1)
                                n += 1

                def add_product(eng, b, j, n, into, g):
                    t = b * TB + 2 * j
                    v = into[:, t:t + 2, :]
                    eng.wait_ge(s_y, n + 1)
                    p = ps[:, 3 + n % 2, :].rearrange("p (t d) -> p t d", t=2)
                    if g is None:
                        eng.tensor_tensor(v, p, v, ALU.add).then_inc(s_yfree, 1)
                    else:
                        if n >= 2:
                            eng.wait_ge(s_x, n - 1)
                        eng.tensor_tensor(gated_y[:, n % 2, :, :], p, g.to_broadcast([P, 2, D]), ALU.mult).then_inc(s_yfree, 1)
                        eng.wait_ge(s_yfree, n + 1)
                        eng.tensor_tensor(v, v, gated_y[:, n % 2, :, :], ALU.add).then_inc(s_x, 1)

                @blk.vector
                def _(eng):
                    eng.wait_ge(ld["x"], 16)
                    eng.wait_ge(ld["small"], 32)
                    n = i_qk = 0
                    for i in range(0, NBLK + 3):
                        b = i - 1
                        if here(b):
                            if OUT:
                                eng.wait_ge(s_b, b + 1)
                                for j in range(2):
                                    add_product(eng, b, j, y_event(b, False, j), src,
                                                None if gk is None else gate[:, b // 2, gk:gk + 1, :])
                                eng.wait_ge(s_yfree if gk is None else s_x, y_event(b, False, 1) + 1)
                            for t in range(b * TB, (b + 1) * TB):
                                eng.bn_stats(st[:, t, :], src[:, t, :]).then_inc(s_stat, 1)
                            for t in range(b * TB, (b + 1) * TB):
                                eng.wait_ge(s_stat, t + 1)
                                eng.bn_aggr(mv[:, t, :], st[:, t, :]).then_inc(s_var, 1)
                            eng.wait_ge(s_std, b + 1)
                            eng.reciprocal(rstd[:, b * TB:(b + 1) * TB], std[:, b * TB:(b + 1) * TB]).then_inc(s_rstd, 1)
                            eng.wait_ge(s_rstd, b + 1)
                            for t in range(b * TB, (b + 1) * TB):
                                eng.tensor_scalar(h[:, t, :], src[:, t, :], mv[:, t, 0:1], rstd[:, t:t + 1],
                                                  ALU.subtract, ALU.mult).then_inc(s_h, 1)
                        if projected is not None:
                            for job in jobs_of.get(i, ()):
                                if job[0] == "qk":
                                    _, _, _, col, _, _, nt = job
                                    buf = i_qk % NPART
                                    if i_qk >= NPART:
                                        eng.wait_ge(s_q3, i_qk - NPART + 1)
                                    eng.wait_ge(s_q1, i_qk + 1)
                                    eng.scalar_tensor_tensor(out=rest[:, buf, 0:nt], in0=ps[:, bank(n), 0:nt],
                                                             scalar=cols[:, col:col + 1], in1=parts[:, buf, 0, 0:nt],
                                                             op0=ALU.add, op1=ALU.subtract).then_inc(s_pjfree, 1)
                                    eng.wait_ge(s_pjfree, n + 1)
                                    eng.tensor_copy(parts[:, buf, 1, 0:nt], rest[:, buf, 0:nt]).then_inc(s_q2, 1)
                                    i_qk += 1
                                else:
                                    _, _, _, row, tt, nt, at = job
                                    eng.wait_ge(s_pj, n + 1)
                                    eng.tensor_tensor(at(v_all, nt), ps[0:nt, bank(n), 0:D].rearrange("p (g f) -> p g f", g=G),
                                                      rows[0:nt, row, :].rearrange("p (g f) -> p g f", g=G),
                                                      ALU.add).then_inc(s_pjfree, 1)
                                n += 1
                        elif here(i - 3):
                            b = i - 3
                            eng.wait_ge(s_xb, b + 1)
                            for j in range(2):
                                add_product(eng, b, j, y_event(b, True, j), xs, gate[:, b // 2, 2:3, :] if mgate else None)

                @blk.gpsimd
                def _(eng):
                    stage.clear_before(eng)
                    if OUT:
                        eng.wait_ge(ld["x"], 16)
                        for b in range(NBLK):
                            t0, t1 = b * TB, (b + 1) * TB
                            eng.tensor_tensor(src[:, t0:t1, :], xs[:, t0:t1, :], bias(b // 2).to_broadcast([P, TB, D]),
                                              ALU.add).then_inc(s_b, 1)
                    if projected is not None:
                        for i, job in enumerate(job for _, job in jobs if job[0] == "qk"):
                            nt, buf = job[6], i % NPART
                            eng.wait_ge(s_q2, i + 1)
                            if i >= NPART:
                                eng.wait_ge(s_stored[buf], 16 * (i // NPART))
                            eng.tensor_tensor(parts[:, buf, 2, 0:nt], rest[:, buf, 0:nt], parts[:, buf, 1, 0:nt],
                                              ALU.subtract).then_inc(s_q3, 1)
                    else:
                        for b in range(NBLK):
                            t0, t1 = b * TB, (b + 1) * TB
                            r = gbias[:, b // 2, 2:3, :] if mgate else rows[:, ROW["ff2_b"]:ROW["ff2_b"] + 1, :]
                            eng.wait_ge(s_h, t1)
                            eng.tensor_tensor(xs[:, t0:t1, :], xs[:, t0:t1, :], r.to_broadcast([P, TB, D]),
                                              ALU.add).then_inc(s_xb, 1)

                @blk.sync
                def _(eng):
                    if projected is not None:
                        stored = [0] * NPART
                        for i, job in enumerate(job for _, job in jobs if job[0] == "qk"):
                            _, _, _, _, dst, (_, t0), nt = job
                            buf = i % NPART
                            eng.wait_ge(s_q3, i + 1)
                            eng.dma_start(dst[:, :, t0:t0 + nt], parts[:, buf, :, 0:nt]).then_inc(s_stored[buf], 16)
                            stored[buf] += 16
                        for buf in range(NPART):
                            eng.wait_ge(s_stored[buf], stored[buf])
                    else:
                        eng.dma_start(wf1[:, :, :], chunked(w1)).then_inc(ld[s_w1], 16)
                        eng.dma_start(wf2[:, :, :], chunked(w2)).then_inc(ld[s_w2], 16)
                        if final:
                            for n in range(2 * NBLK):
                                eng.wait_ge(s_x, y_event(n // 2, True, n % 2) + 1)
                                eng.dma_start(out.rearrange("(t p) d -> p t d", p=P)[:, 2 * n:2 * n + 2, :],
                                              xs[:, 2 * n:2 * n + 2, :]).then_inc(s_out, 16)
                            eng.wait_ge(s_out, 16 * 2 * NBLK)
            stage.end()

        def attention_stage(a, qd, kd, loads=()):
            stage = Stage()
            sem = stage.sem
            tag = a.name
            s_qk, s_v, s_ones = sem("qk_loaded" + tag), sem("values_ready" + tag), sem("ones_ready" + tag)
            s_a, s_max, s_m = sem("max_scores_ready" + tag), sem("max_bank_done" + tag), sem("max_parts" + tag)
            s_sc, s_ex, s_pv = sem("scores_ready" + tag), sem("exp_done" + tag), sem("pv_done" + tag)
            s_warm = sem("table_loaded" + tag)
            s_acc, s_inv = sem("accumulator_moved" + tag), sem("sums_inverted" + tag)
            PV0 = 2
            MC = 6
            with ExitStack() as tmp:
                Q = sb("Q" + tag, [P, 2, HG, a.NQ], BF16, tmp)
                K = sb("K" + tag, [P, 2, HG, a.NK], BF16, tmp)
                V = sb("V" + tag, [P, a.KT, HG, 32], FP32, tmp)
                NE = 2 + a.KT % 2
                E = sb("E" + tag, [P, NE, HG, BLK], FP32, tmp)
                O = sb("O" + tag, [P, BLK], FP32, tmp)
                mx = sb("mx" + tag, [P, a.NI, a.NKB], FP32, tmp)
                nm = sb("nm" + tag, [P, a.NI], FP32, tmp)
                nr = sb("nr" + tag, [P, 2, a.NI], FP32, tmp)
                mp = sb("mp" + tag, [P, a.NI, KM], BF16, tmp)
                inv = sb("inv" + tag, [P, HG * TB], FP32, tmp)
                otok = hT[:, :, :].rearrange("p c (t n) -> p (c t) n", n=D)
                warm = sb("warm" + tag, [P, 1], FP32, tmp)
                blk = tmp.enter_context(nc.Block())

                def ebuf(s):
                    return 2 if s == a.KT - 1 and a.KT % 2 else s % 2

                @blk.sync
                def _(eng):
                    def load(j, par):
                        for r in range(len(Q_PARTS)):
                            for buf, src, part in ((Q, qd, Q_PARTS[r]), (K, kd, K_PARTS[r])):
                                eng.dma_start(buf[DK * r:DK * (r + 1), par, :, :].rearrange("p a h t -> p (a h) t"),
                                              src[j, :, part, :].rearrange("a (h f) t -> f (a h) t", f=DK)).then_inc(s_qk, 16)

                    def loaded(j):
                        return 16 * 2 * len(Q_PARTS) * (j + 1)

                    load(ds(0, 1), ds(0, 1))
                    eng.wait_ge(s_qk, loaded(0))
                    load(ds(1, 1), ds(1, 1))
                    for dst, src, s in loads:
                        eng.dma_start(dst[:, :, :], chunked(src)).then_inc(ld[s], 16)
                    with eng.Fori(0, a.J - 2) as j:
                        eng.wait_ge(s_acc, (j + 1) * a.NB)
                        eng.wait_ge(s_qk, loaded(j + 1))
                        load(ds(j + 2, 1), ds(j % 2, 1))

                @blk.gpsimd
                def _(eng):
                    stage.clear_before(eng)
                    eng.memset(V[:, :, :, DK:32], 1.0).then_inc(s_ones, 1)
                    eng.wait_ge(s_ones, 1)
                    eng.memset(K[KQ:KQ + KM, :, :, :], 1.0).then_inc(s_ones, 1)
                    eng.wait_ge(s_ones, 2)

                    def values(c, base):
                        k0, k1 = c * a.VC, min((c + 1) * a.VC, a.KT)
                        full = [k for k in range(k0, k1) if a.KW[k] == P]
                        for lo, n, wd in ((k0, len(full), P), (k0 + len(full), k1 - k0 - len(full), a.KW[-1])):
                            if n:
                                last = eng.tensor_copy(V[0:wd, lo:lo + n, :, 0:DK],
                                                       v_all[0:wd, ds(base + lo, n), :].rearrange("p k (h f) -> p k h f", h=HG))
                        last.then_inc(s_v, 1)

                    for c in range(a.NVC):
                        values(c, 0)
                    with eng.Fori(1, a.J) as j:
                        for c in range(a.NVC):
                            eng.wait_ge(s_pv, PV0 + (j * a.NB - 1) * a.KT + min((c + 1) * a.VC, a.KT))
                            values(c, j * a.KT)

                def find_max(eng, u, k):
                    bank = 5 + place(u, k) % 3
                    i, kb = k // a.NKB, k % a.NKB
                    h, qt = i // TB, i % TB
                    j, b = u // a.NB, u % a.NB
                    return eng.matmul(ps[:, bank, 0:a.KBW[kb]],
                                      Q[0:KQ, ds(j % 2, 1), h, ds(b * BLK + qt * P, P)].rearrange("p a t -> p (a t)"),
                                      K[0:KQ, ds(j % 2, 1), h, kb * BLK:kb * BLK + a.KBW[kb]].rearrange("p a t -> p (a t)"),
                                      start=True, stop=True)

                searches = a.KT - a.AHEAD
                TURN_STEP = 2
                TURN = a.L + (a.NA - a.L) * (TURN_STEP + 1) // searches

                def before_unit(v):
                    return v * a.NA if isinstance(v, int) and v < 2 else v * (a.NA + 1) - 2

                def place(v, k):
                    return k + (not (isinstance(v, int) and v < 2) and k >= TURN)

                def last_use(r, size):
                    return r - 3 if r >= 3 else max(n for n in range(size) if n % 3 == r) - size

                def stage_block(u):
                    return u // a.NB, u % a.NB

                @blk.tensor
                def _(eng):
                    def free_bank(v, r, size):
                        eng.wait_ge(s_max, before_unit(v) + last_use(r, size) + 1)

                    def search(v, k, first=False):
                        if not (first and k < 3):
                            free_bank(v, place(v, k), a.NA if isinstance(v, int) and v <= 2 else a.NA + 1)
                        find_max(eng, v, k).then_inc(s_a, 1)

                    def turn(w, v, r):
                        eng.wait_ge(s_acc, w + 1)
                        free_bank(v, r, a.NA + 1)
                        for t in range(TB):
                            last = eng.transpose(ps[:, 5 + r % 3, t * P:(t + 1) * P], O[:, t * P:(t + 1) * P], ident[:, :])
                        last.then_inc(s_a, 1)

                    def lay_maxima(u, event):
                        eng.wait_ge(s_m, MC * (u + 1))
                        for p in range(2):
                            if event is not None:
                                eng.wait_ge(s_ex, event + p - 1)
                            for h in range(2):
                                for qt in range(TB):
                                    last = eng.matmul(ps[KQ:KQ + KM, 2 * p + h, qt * P:(qt + 1) * P],
                                                      mp[:, (2 * p + h) * TB + qt, :], identb[:, :], start=True, stop=True)
                            last.then_inc(s_sc, 1)

                    def scores(u, s, event, p):
                        j, b = u // a.NB, u % a.NB
                        eng.wait_ge(s_ex, event + p - 1)
                        for h in range(2 * p, 2 * p + 2):
                            last = eng.matmul(ps[0:a.KW[s], h, :],
                                              K[0:KQ + KM, ds(j % 2, 1), h, s * P:s * P + a.KW[s]].rearrange("p a t -> p (a t)"),
                                              Q[0:KQ + KM, ds(j % 2, 1), h, ds(b * BLK, BLK)].rearrange("p a t -> p (a t)"),
                                              start=True, stop=True)
                        last.then_inc(s_sc, 1)

                    def weigh(u, s, event, first):
                        if s == 0 and not first:
                            eng.wait_ge(s_acc, u)
                        eng.wait_ge(s_ex, event + 2)
                        if s % a.VC == 0:
                            eng.wait_ge(s_v, (u // a.NB) * a.NVC + s // a.VC + 1)
                        for h in range(HG):
                            last = eng.matmul(ps[32 * h:32 * h + 32, 4, :], V[0:a.KW[s], s, h, :], E[0:a.KW[s], ebuf(s), h, :],
                                              start=(s == 0), stop=(s == a.KT - 1))
                        last.then_inc(s_pv, 1)

                    def unit(u, first=False, left=2):
                        n = u * a.EV + 2
                        for s in range(a.KT):
                            if s < searches:
                                lo, hi = (a.L + (a.NA - a.L) * (s + i) // searches for i in range(2))
                                beside = [(u + 1, k) for k in range(lo, hi)] if left >= 1 else []
                            else:
                                lo, hi = (a.L * (s - searches + i) // a.AHEAD for i in range(2))
                                beside = [(u + 2, k) for k in range(lo, hi)] if left >= 2 else []
                            if s == searches and left >= 2:
                                eng.wait_ge(s_qk, LOADED * ((u + 2) // a.NB + 1))
                            if s == a.M_STEP and left >= 1:
                                lay_maxima(u + 1, n)
                                n += 2
                                for v, k in beside[:2]:
                                    search(v, k)
                                beside = beside[2:]
                            scores(u, s, n, 0)
                            for v, k in beside[:1]:
                                search(v, k)
                            scores(u, s, n, 1)
                            for v, k in beside[1:2]:
                                search(v, k)
                            if s > 0:
                                weigh(u, s - 1, before, first)
                            elif not first:
                                weigh(u - 1, a.KT - 1, n - 2, False)
                            for v, k in beside[2:]:
                                search(v, k)
                            if s == TURN_STEP and not first:
                                if left >= 1:
                                    turn(u - 1, u + 1, TURN)
                                else:
                                    turn(u - 1, a.U, 0)
                            before = n
                            n += 2

                    LOADED = 16 * 2 * len(Q_PARTS)
                    eng.sem_inc(s_pv, PV0)
                    eng.wait_ge(s_ones, 2)
                    eng.wait_ge(s_qk, LOADED)
                    for k in range(a.NA):
                        search(0, k, first=True)
                    for k in range(a.L):
                        search(1, k)
                    lay_maxima(0, None)
                    unit(0, first=True)
                    with eng.Fori(1, a.U - 2) as u:
                        unit(u)
                    unit(a.U - 2, left=1)
                    unit(a.U - 1, left=0)
                    weigh(a.U - 1, a.KT - 1, (a.U - 1) * a.EV + 2 * a.KT, False)
                    turn(a.U - 1, a.U, 1)

                @blk.scalar
                def _(eng):
                    def expose(u, s, event):
                        for p in range(2):
                            eng.wait_ge(s_sc, event + p + 1)
                            if p == 0:
                                eng.wait_ge(s_pv, PV0 + u * a.KT + s - 1)
                            eng.activation(E[0:a.KW[s], ebuf(s), 2 * p:2 * p + 2, :], ps[0:a.KW[s], 2 * p:2 * p + 2, :],
                                           ACT.Exp, scale=SCALE).then_inc(s_ex, 1)

                    def place_maxima(u, event):
                        j, b = u // a.NB, u % a.NB
                        for p in range(2):
                            eng.wait_ge(s_sc, event + p + 1)
                            eng.activation(Q[KQ:KQ + KM, ds(j % 2, 1), 2 * p:2 * p + 2, ds(b * BLK, BLK)].rearrange("p a h t -> p (a h) t"),
                                           ps[KQ:KQ + KM, 2 * p:2 * p + 2, :], ACT.Copy).then_inc(s_ex, 1)

                    def move_out(u, first=False, last=False):
                        eng.wait_ge(s_pv, PV0 + (u + 1) * a.KT)
                        if not first:
                            eng.wait_ge(s_a, before_unit(u + 1) + (0 if last else TURN) + 1)
                        eng.activation(O[:, :], ps[:, 4, :], ACT.Copy).then_inc(s_acc, 1)

                    def unit(u, index=None, last=False):
                        n = u * a.EV + 2
                        for s in range(a.KT):
                            if s == a.M_STEP and not last:
                                place_maxima(u + 1, n)
                                n += 2
                            expose(u, s, n)
                            n += 2
                            if s == 0 and index != 0:
                                move_out(u - 1, index == 1)

                    eng.activation(warm[:, :], eps[:, 0:1], ACT.Exp).then_inc(s_warm, 1)
                    place_maxima(0, 0)
                    unit(0, 0)
                    unit(1, 1)
                    with eng.Fori(2, a.U - 1) as u:
                        unit(u)
                    unit(a.U - 1, last=True)
                    move_out(a.U - 1, last=True)

                @blk.vector
                def _(eng):
                    def reduce(v, k):
                        i, kb = k // a.NKB, k % a.NKB
                        r = place(v, k)
                        eng.wait_ge(s_a, before_unit(v) + r + 1)
                        eng.tensor_reduce(mx[:, i, kb:kb + 1], ps[:, 5 + r % 3, 0:a.KBW[kb]], AX.X, ALU.max).then_inc(s_max, 1)

                    def divide(w, v, r):
                        j, b = stage_block(w)
                        g, tile = (j, b * TB) if a.J == G else (j % G, (j // G) * (a.NQ // P) + b * TB)
                        eng.wait_ge(s_a, before_unit(v) + r + 1)
                        acc = ps[:, 5 + r % 3, :].rearrange("p (t h c) -> p t h c", t=TB, h=HG)
                        eng.reciprocal(inv[:, :].rearrange("p (t h) -> p t h", t=TB), acc[:, :, :, DK]).then_inc(s_inv, 1)
                        eng.wait_ge(s_inv, w + 1)
                        eng.tensor_tensor(otok[:, ds(tile, TB), ds(g * GW, GW)].rearrange("p t (h f) -> p t h f", h=HG),
                                          acc[:, :, :, 0:DK],
                                          inv[:, :].rearrange("p (t h a) -> p t h a", t=TB, a=1).to_broadcast([P, TB, HG, DK]),
                                          ALU.mult).then_inc(s_max, 1)

                    def maxima(v):
                        for k in range(a.NA):
                            if k == TURN and not (isinstance(v, int) and v < 2):
                                divide(v - 2, v, TURN)
                            reduce(v, k)
                        m = v * MC
                        eng.wait_ge(s_max, before_unit(v) + place(v, a.NA - 1) + 1)
                        eng.tensor_reduce(nm[:, :], mx[:, :, :], AX.X, ALU.max, negate=True).then_inc(s_m, 1)
                        eng.wait_ge(s_m, m + 1)
                        eng.tensor_copy(mp[:, :, 0], nm[:, :]).then_inc(s_m, 1)
                        eng.wait_ge(s_m, m + 2)
                        eng.tensor_tensor(nr[:, 0, :], nm[:, :], mp[:, :, 0], ALU.subtract).then_inc(s_m, 1)
                        eng.wait_ge(s_m, m + 3)
                        eng.tensor_copy(mp[:, :, 1], nr[:, 0, :]).then_inc(s_m, 1)
                        eng.wait_ge(s_m, m + 4)
                        eng.tensor_tensor(nr[:, 1, :], nr[:, 0, :], mp[:, :, 1], ALU.subtract).then_inc(s_m, 1)
                        eng.wait_ge(s_m, m + 5)
                        eng.tensor_copy(mp[:, :, 2], nr[:, 1, :]).then_inc(s_m, 1)

                    maxima(0)
                    maxima(1)
                    with eng.Fori(2, a.U) as v:
                        maxima(v)
                    divide(a.U - 2, a.U, 0)
                    eng.wait_ge(s_max, before_unit(a.U) + 1)
                    divide(a.U - 1, a.U, 1)
            stage.end()

        def part_rows(dst, a, c, t0):
            half = t0 // a.NQ if a.J > G else 0
            j = half * G + c * (P // GW)
            return dst[j:j + P // GW].rearrange("j f r t -> (j f) r t"), t0 - half * (S // 2 if a.J > G else 0)

        def v_place(a, tt, swap):
            if a.J == G:
                return lambda v, nt: v[0:nt, 0:a.J * a.KT, :].rearrange("p (g k) f -> p g k f", g=G)[:, :, tt, :]
            half = tt // a.KT ^ swap
            return lambda v, nt: v[0:nt, half * G * a.KT:(half + 1) * G * a.KT, :]\
                .rearrange("p (g k) f -> p g k f", g=G)[:, :, tt % a.KT, :]

        def projections(a, n, wt, wload, qcol, vrow, swap=0):
            def jobs_of(src):
                jobs = {}
                for b in range(NBLK):
                    jobs[b + 3] = []
                    for which, dst in ((0, q_dram[n]), (1, k_dram[n])):
                        for c in range(KC):
                            rows_, t0 = part_rows(dst, a, c, b * BLK)
                            if which and swap:
                                rows_, _ = part_rows(dst, a, c, (b * BLK + S // 2) % S)
                            o = which * D + c * P
                            jobs[b + 3].append(("qk", src, ((lambda kc, o=o: wt[:, kc, o:o + P]), wload),
                                                qcol + which * KC + c, rows_, (b * BLK, t0), BLK))
                    for t in range(TB):
                        jobs[b + 3].append(("v", src, ((lambda kc: wt[:, kc, 2 * D:3 * D]), wload), vrow, b * TB + t, P,
                                            v_place(a, b * TB + t, swap)))
                return jobs
            return jobs_of

        def cross_projections(src):
            a = attn[1]
            jobs = {i: [] for i in range(NBLK + 3)}
            wload = (("wcq", 48), ("ctx", 16))
            for b in range((SC + BLK - 1) // BLK):
                nt = min(BLK, SC - b * BLK)
                at = min(b, 2)
                for c in range(KC):
                    rows_, _ = part_rows(k_dram[1], a, c, 0)
                    o = D + c * P
                    jobs[at].append(("qk", cT, ((lambda kc, o=o: wcq[:, kc, o:o + P]), wload), COL["ck_b"] + c, rows_,
                                     (b * BLK, b * BLK), nt))
                for tt in range(b * TB, min((b + 1) * TB, a.KT)):
                    jobs[at].append(("v", cT, ((lambda kc: wcq[:, kc, 2 * D:3 * D]), wload), ROW["cv_b"], tt, a.KW[tt],
                                     v_place(a, tt, 0)))
            for b in range(NBLK):
                for c in range(KC):
                    rows_, _ = part_rows(q_dram[1], a, c, 0)
                    jobs[b + 3].append(("qk", src, ((lambda kc, o=c * P: wcq[:, kc, o:o + P]), wload), COL["cq_b"] + c, rows_,
                                        (b * BLK, b * BLK), BLK))
            return jobs

        def col(name):
            return lambda kc, half: cols[:, COL[name] + kc:COL[name] + kc + 1]

        def modulation(k):
            return (lambda kc, half: shift[:, 2 * (2 * k + 1) + kc, half:half + 1],
                    lambda kc, half: shift[:, 2 * (2 * k) + kc, half:half + 1])

        def row(name):
            return lambda half: rows[:, ROW[name]:ROW[name] + 1, :]

        def gated_row(k):
            return lambda half: gbias[:, half, k:k + 1, :]

        dense_stage("d0", 0, col("ln1_g"), col("ln1_b"),
                    projections(attn[0], 0, wq, (("wq", 16),), COL["in_b"], ROW["v_b"]))
        attention_stage(attn[0], q_dram[0], k_dram[0])
        dense_stage("d1", 0, col("ln2_g"), col("ln2_b"), cross_projections, attended=(wo, "wo", row("out_b"), None))
        attention_stage(attn[1], q_dram[1], k_dram[1],
                        ((wq, w["qkv2"], "wq2"), (wo, w["proj2"], "wo2"), (wcq, w["cqkv2"], "wcq2")))
        dense_stage("d2", 0, col("ln3_g"), col("ln3_b"), attended=(wco, "wco", row("co_b"), None),
                    mlp=(COL["ff1_b"], ACT.Gelu, False, (w["ff1"], w["ff2"]), ("wf1", "wf2"), False))

        dense_stage("d3", 1, *modulation(0), projections(attn[2], 2, wq, (("wq2", 16),), COL["qkv2_b"], ROW["v2_b"]))
        attention_stage(attn[2], q_dram[2], k_dram[2], ((wco, w["cproj2"], "wco2"),))
        dense_stage("d4", 1, *modulation(1), projections(attn[3], 3, wcq, (("wcq2", 16),), COL["cqkv2_b"], ROW["cv2_b"], 1),
                    attended=(wo, "wo2", gated_row(0), 0), mid=True)
        attention_stage(attn[3], q_dram[3], k_dram[3])
        dense_stage("d5", 1, *modulation(2), attended=(wco, "wco2", gated_row(1), 1),
                    mlp=(COL["fc1_b"], ACT.Gelu_apprx_tanh, True, (w["fc12"], w["fc22"]), ("wf12", "wf22"), True))


def kernel(**inputs):
    import numpy as np
    import concourse.bacc as bacc
    from concourse.bass_utils import run_bass_kernel_spmd

    a = {k: np.asarray(v) for k, v in inputs.items()}
    L0, L1 = "L0_xattn_", "L1_xattn_"

    def t(name):
        return np.ascontiguousarray(a[name].T)

    col_at, cols = {}, []
    for name, v in (("ln1_g", a[L0 + "ln1_g"]), ("ln1_b", a[L0 + "ln1_b"]), ("ln2_g", a[L0 + "ln2_g"]),
                    ("ln2_b", a[L0 + "ln2_b"]), ("ln3_g", a[L0 + "ln3_g"]), ("ln3_b", a[L0 + "ln3_b"]),
                    ("in_b", a[L0 + "in_proj_b"]), ("cq_b", a[L0 + "cq_b"]), ("ck_b", a[L0 + "ck_b"]),
                    ("ff1_b", a[L0 + "ff1_b"]), ("qkv2_b", a[L1 + "attn_qkv_b"]), ("cqkv2_b", a[L1 + "crs_qkv_b"]),
                    ("fc1_b", a[L1 + "mlp_fc1_b"]), ("ada_b", a[L1 + "ada_b"])):
        col_at[name] = len(cols)
        cols += list(v.reshape(-1, 128))
    row_at, rows = {}, []
    for name, vs in (("v_b", [a[L0 + "in_proj_b"][512:]]), ("out_b", [a[L0 + "out_proj_b"]]), ("cv_b", [a[L0 + "cv_b"]]),
                     ("co_b", [a[L0 + "co_b"]]), ("ff2_b", [a[L0 + "ff2_b"]]), ("v2_b", [a[L1 + "attn_qkv_b"][512:]]),
                     ("cv2_b", [a[L1 + "crs_qkv_b"][512:]]),
                     ("gate", [a[L1 + "ada_b"][k * 256:(k + 1) * 256] for k in (2, 5, 8)]),
                     ("out2", [a[L1 + "attn_proj_b"], a[L1 + "crs_proj_b"], a[L1 + "mlp_fc2_b"]])):
        row_at[name] = len(rows)
        rows += vs
    arrays = {
        "x": a["x"].reshape(2048, 256), "ctxT": np.ascontiguousarray(a["ctx_1024"][0].T),
        "cols": np.ascontiguousarray(np.stack(cols, 1)), "rows": np.ascontiguousarray(np.stack(rows, 0)),
        "in_proj": t(L0 + "in_proj_w"), "out_proj": t(L0 + "out_proj_w"), "cq": t(L0 + "cq_w"), "ck": t(L0 + "ck_w"),
        "cv": t(L0 + "cv_w"), "co": t(L0 + "co_w"), "ff1": t(L0 + "ff1_w"), "ff2": t(L0 + "ff2_w"),
        "qkv2": a[L1 + "attn_qkv_w"], "proj2": a[L1 + "attn_proj_w"], "cqkv2": a[L1 + "crs_qkv_w"],
        "cproj2": a[L1 + "crs_proj_w"], "fc12": a[L1 + "mlp_fc1_w"], "fc22": a[L1 + "mlp_fc2_w"], "ada": a[L1 + "ada_w"],
    }
    nc = bacc.Bacc("TRN2", target_bir_lowering=False, num_devices=1)
    feeds, w = {}, {}
    for name, v in arrays.items():
        feeds["in_" + name] = np.ascontiguousarray(v)
        w[name] = nc.dram_tensor("in_" + name, v.shape, mybir.dt.from_np(v.dtype), kind="ExternalInput").ap()
    out = nc.dram_tensor("out_0", (2048, 256), FP32, kind="ExternalOutput").ap()
    w["col_at"], w["row_at"] = col_at, row_at
    build(nc, w["x"], w["ctxT"], w, out)
    r = run_bass_kernel_spmd(nc, [feeds], core_ids=[0])
    return r.results[0]["out_0"].reshape(1, 2048, 256)
```

```python
import concourse.bass as bass
from concourse import mybir
from contextlib import ExitStack

FP32 = mybir.dt.float32
BF16 = mybir.dt.bfloat16
ALU = mybir.AluOpType
ACT = mybir.ActivationFunctionType
AX = mybir.AxisListType
ds = bass.ds

P = 128
S = 2048
D = 256
KC = D // P
T = S // P
BLK = 512
NBLK = S // BLK
TB = BLK // P
SC = 1601
H = 16
DK = D // H
HG = 4
G = H // HG
GW = HG * DK
F = 1024
FC = F // P
SCALE = 0.25

Q_PARTS = (0, 0, 0, 1, 1, 2)
K_PARTS = (0, 1, 2, 0, 1, 0)
KQ = len(Q_PARTS) * DK
KM = 3


class Attention:

    def __init__(self, name, stages, queries, keys):
        self.name = name
        self.J = stages
        self.NQ = queries
        self.NK = keys
        self.NB = queries // BLK
        self.U = stages * self.NB
        self.KT = (keys + P - 1) // P
        self.KW = [min(P, keys - P * k) for k in range(self.KT)]
        self.NKB = (keys + BLK - 1) // BLK
        self.KBW = [min(BLK, keys - BLK * k) for k in range(self.NKB)]
        self.NI = HG * TB
        self.NARROW = self.KBW[-1] * TB <= BLK
        self.FULL = self.NKB - self.NARROW
        self.NS = TB * self.FULL + self.NARROW
        self.NA = HG * self.NS
        self.EV = 2 * self.KT
        self.M_STEP = self.KT - 1
        self.AHEAD = 3
        self.L = self.NA * self.AHEAD // self.KT
        self.VC = 4
        self.NVC = (self.KT + self.VC - 1) // self.VC


def build(nc, x, ctxT, w, out):
    ctx = ExitStack()
    with ctx:
        def sb(name, shape, dt=FP32, stack=ctx):
            return stack.enter_context(nc.sbuf_tensor(name, shape, dt))

        def lasting_sem(name):
            return ctx.enter_context(nc.semaphore(name))

        class Stage:
            last = None

            def __init__(self):
                self.stack = ExitStack()
                self.sems = []
                self.before = Stage.last
                Stage.last = self

            def sem(self, name):
                self.sems.append(self.stack.enter_context(nc.semaphore(name)))
                return self.sems[-1]

            def clear_before(self, pool):
                for s in self.before.sems if self.before else ():
                    pool.sem_clear(s)

            def end(self):
                if self.before:
                    self.before.stack.close()

        def dram(name, shape, dt=FP32):
            return nc.dram_tensor(name, shape, dt, kind="Internal").ap()

        xs = sb("xs", [P, T, D])
        hT = sb("hT", [P, KC, S])
        cT = sb("cT", [P, KC, SC])
        v_all = sb("v_all", [P, 64, GW])
        ident = sb("ident", [P, P])
        identb = sb("identb", [P, P], BF16)
        wq = sb("wq", [P, KC, 3 * D])
        wo = sb("wo", [P, KC, D])
        wcq = sb("wcq", [P, KC, 3 * D])
        wco = sb("wco", [P, KC, D])
        cols = sb("cols", [P, w["cols"].shape[1]])
        rows = sb("rows", [P, w["rows"].shape[0], D])
        shift = sb("shift", [P, 12, 2])
        gate = sb("gate", [P, 2, 3, D])
        gbias = sb("gbias", [P, 2, 3, D])
        eps = sb("eps", [P, 2])
        O = sb("O", [P, BLK])
        sums = sb("sums", [P, DK])
        inverse = sb("inverse", [P, BLK])
        ps = ctx.enter_context(nc.psum_tensor("ps", [P, 8, BLK], FP32))
        until_modulation = ExitStack()
        zero = sb("zero", [P, P], FP32, until_modulation)

        COL = w["col_at"]
        ROW = w["row_at"]

        attn = [Attention("a0", G, S, S), Attention("a1", G, S, SC),
                Attention("a2", 2 * G, S // 2, S // 2), Attention("a3", 2 * G, S // 2, S // 2)]
        q_dram = [dram(f"q_parts{a.name}", [a.J, GW, 3, a.NQ], BF16) for a in attn]
        k_dram = [dram(f"k_parts{a.name}", [a.J, GW, 3, a.NK], BF16) for a in attn]

        ld = {n: lasting_sem("ld_" + n) for n in ("x0", "x1", "x2", "x3", "ctx", "cols", "rows", "wq", "wo", "wcq", "wco", "wf1", "wf2", "ada",
                                          "wq2", "wo2", "wcq2", "wco2", "wf12", "wf22")}
        s_id = lasting_sem("identities_made")

        def chunked(ap):
            return ap.rearrange("(c p) n -> p c n", p=P)

        stage = Stage()
        with nc.Block() as blk:

            @blk.sync
            def _(eng):
                eng.dma_start(cols[:, :], w["cols"]).then_inc(ld["cols"], 16)
                for b in range(NBLK):
                    eng.dma_start(xs[:, b * TB:(b + 1) * TB, :], x.rearrange("(t p) d -> p t d", p=P)[:, b * TB:(b + 1) * TB, :])\
                        .then_inc(ld[f"x{b}"], 16)
                eng.dma_start(rows[:, :, :], w["rows"].partition_broadcast(P)).then_inc(ld["rows"], 16)
                eng.dma_start(cT[:, :, :], chunked(ctxT)).then_inc(ld["ctx"], 16)
                eng.dma_start(wo[:, :, :], chunked(w["out_proj"])).then_inc(ld["wo"], 16)
                for i, n in enumerate(("cq", "ck", "cv")):
                    eng.dma_start(wcq[:, :, i * D:(i + 1) * D], chunked(w[n])).then_inc(ld["wcq"], 16)
                eng.dma_start(wco[:, :, :], chunked(w["co"])).then_inc(ld["wco"], 16)

            @blk.scalar
            def _(eng):
                eng.dma_start(wq[:, :, :], chunked(w["in_proj"])).then_inc(ld["wq"], 16)

            @blk.gpsimd
            def _(eng):
                eng.memset(ident[:, :], 0.0).then_inc(s_id, 1)
                eng.memset(identb[:, :], 0.0).then_inc(s_id, 1)
                eng.memset(zero[:, :], 0.0).then_inc(s_id, 1)
                eng.memset(eps[:, 0:1], 1e-5).then_inc(s_id, 1)
                eng.memset(eps[:, 1:2], 1e-6).then_inc(s_id, 1)
                eng.wait_ge(s_id, 2)
                for m in (ident, identb):
                    eng.affine_select(out=m[:, :], in_=m[:, :], compare_op=ALU.not_equal, fill=1.0,
                                      base=0, pattern=[[-1, P]], channel_multiplier=1).then_inc(s_id, 1)
        stage.end()

        class Modulation:
            VECS = (0, 1, 3, 4, 6, 7)
            GATES = (2, 5, 8)
            NV = len(VECS) * KC
            N = NV + 2 * len(GATES)

            def __init__(self, sem, sb, spare):
                nv = KC * len(self.VECS) * D
                spare = spare[:, :, :, :].rearrange("p e h n -> p (e h n)")
                self.vec_w = spare[:, 0:nv].rearrange("p (c n) -> p c n", c=KC)
                self.silr = spare[:, nv:nv + KC * 2 * P].rearrange("p (c h n) -> p c h n", c=KC, h=2)
                self.gate_w = sb("gate_weights", [P, KC, len(self.GATES), D])
                self.sil = sb("silu_c", [P, KC, 2])
                self.s_silu, self.s_products, self.s_moved, self.s_done = (
                    sem(n) for n in ("silu_done", "modulation_products", "modulation_moved", "modulation_done"))

            def load(self, eng):
                ada = chunked(w["ada"])
                for k, v in enumerate(self.GATES):
                    eng.dma_start(self.vec_w[:, :, 2 * k * D:2 * (k + 1) * D], ada[:, :, (v - 2) * D:v * D]).then_inc(ld["ada"], 16)
                    eng.dma_start(self.gate_w[:, :, k, :], ada[:, :, v * D:(v + 1) * D]).then_inc(ld["ada"], 16)

            def silu(self, eng):
                eng.wait_ge(ld["ctx"], 16)
                eng.activation(self.sil[:, :, :], cT[:, :, 0:2], ACT.Silu).then_inc(self.s_silu, 1)
                eng.wait_ge(self.s_silu, 1)
                eng.wait_ge(s_id, 3)
                for kc in range(KC):
                    for half in range(2):
                        eng.activation(self.silr[:, kc, half, :], zero[:, :], ACT.Identity,
                                       bias=self.sil[:, kc, half:half + 1]).then_inc(self.s_silu, 1)

            def product(self, eng, n):
                if n == 0:
                    eng.wait_ge(ld["ada"], 16 * 2 * len(self.GATES))
                    eng.wait_ge(self.s_silu, 1 + 2 * KC)
                for kc in range(KC):
                    if n < self.NV:
                        out_, lhsT, rhs = ps[:, 0, 2 * n:2 * n + 2], self.vec_w[:, kc, n * P:(n + 1) * P], self.sil[:, kc, :]
                    else:
                        half, k = (n - self.NV) // 3, (n - self.NV) % 3
                        out_, lhsT, rhs = ps[:, 1 + k, half * D:(half + 1) * D], self.silr[:, kc, half, :], self.gate_w[:, kc, k, :]
                    last = eng.matmul(out_, lhsT, rhs, start=(kc == 0), stop=(kc == KC - 1))
                last.then_inc(self.s_products, 1)

            def move(self, eng):
                eng.wait_ge(ld["cols"], 16)
                eng.wait_ge(self.s_products, self.NV)
                for n in range(self.NV):
                    b = COL["ada_b"] + 2 * self.VECS[n // KC] + n % KC
                    eng.activation(shift[:, n, :], ps[:, 0, 2 * n:2 * n + 2], ACT.Identity,
                                   bias=cols[:, b:b + 1]).then_inc(self.s_moved, 1)
                eng.wait_ge(self.s_products, self.N)
                for n in range(self.NV, self.N):
                    half, k = (n - self.NV) // 3, (n - self.NV) % 3
                    eng.activation(gate[:, half, k, :], ps[:, 1 + k, half * D:(half + 1) * D], ACT.Copy).then_inc(self.s_moved, 1)

            def finish(self, eng):
                eng.wait_ge(ld["rows"], 16)
                eng.wait_ge(self.s_moved, self.N)
                scales = shift[:, :, :].rearrange("p (i v c) h -> p i v (c h)", v=2, c=KC)[:, :, 1, :]
                eng.tensor_scalar(scales, scales, 1.0, None, ALU.add).then_inc(self.s_done, 1)
                eng.wait_ge(self.s_done, 1)
                for half in range(2):
                    eng.tensor_tensor(gate[:, half, :, :], gate[:, half, :, :], rows[:, ROW["gate"]:ROW["gate"] + 3, :],
                                      ALU.add).then_inc(self.s_done, 1)
                    eng.wait_ge(self.s_done, 2 + 2 * half)
                    eng.tensor_tensor(gbias[:, half, :, :], gate[:, half, :, :], rows[:, ROW["out2"]:ROW["out2"] + 3, :],
                                      ALU.mult).then_inc(self.s_done, 1)
                    eng.wait_ge(self.s_done, 3 + 2 * half)

        def v_place(a, tt, nt, swap):
            half = tt // a.KT ^ swap
            return v_all[0:nt, half * G * a.KT:(half + 1) * G * a.KT, :].rearrange("p (g k) f -> p g k f", g=G)[:, :, tt % a.KT, :]

        EARLY = 8

        class Values:

            def __init__(self, a, src, wt, bias, swap):
                self.a, self.src, self.wt, self.bias, self.swap = a, src, wt, bias, swap
                self.tiles = a.KT * (2 if a.J > G else 1)

            def product(self, eng, tt, bank):
                nt = self.a.KW[tt % self.a.KT]
                for kc in range(KC):
                    last = eng.matmul(ps[0:nt, bank, 0:D], self.src[:, kc, tt * P:tt * P + nt], self.wt[:, kc, 2 * D:3 * D],
                                      start=(kc == 0), stop=(kc == KC - 1))
                return last

            def move(self, eng, tt, bank):
                nt = self.a.KW[tt % self.a.KT]
                return eng.tensor_tensor(v_place(self.a, tt, nt, self.swap), ps[0:nt, bank, 0:D].rearrange("p (g f) -> p g f", g=G),
                                         rows[0:nt, self.bias, :].rearrange("p (g f) -> p g f", g=G), ALU.add)

        def dense_stage(tag, e, scale_at, shift_at, projected=None, mlp=None, attended=None, mid=False, values=None):
            stage = Stage()
            sem = stage.sem
            s_stat, s_var, s_std, s_rstd = (sem(n + tag) for n in ("bn_stats_done", "variance_done", "std_done", "rstd_done"))
            s_h, s_tp, s_ev = (sem(n + tag) for n in ("normed_ready", "transposed_ready", "transposed_moved"))
            s_pj, s_pjfree = sem("projected_ready" + tag), sem("projection_bank_free" + tag)
            s_y, s_yfree, s_g, s_x, s_b = (sem(n + tag) for n in ("token_major_ready", "token_major_bank_free", "gated",
                                                                  "residual_done", "bias_added"))
            OUT = attended is not None
            with ExitStack() as tmp:
                st = sb("st" + tag, [P, T, 6], FP32, tmp)
                mv = sb("mv" + tag, [P, T, 2], FP32, tmp)
                std = sb("std" + tag, [P, T], FP32, tmp)
                rstd = sb("rstd" + tag, [P, T], FP32, tmp)
                h = sb("h" + tag, [P, T, D], FP32, tmp)
                gated_y = sb("gated_y" + tag, [P, 2, 2, D], FP32, tmp)
                src = xs
                if OUT:
                    wt, wload, bias, gk, tail = attended
                    if mid:
                        src = sb("xmid" + tag, [P, T, D], FP32, tmp)
                NPART = 8
                if projected is not None:
                    jobs_of = projected
                    jobs = [(i, job) for i in sorted(jobs_of) for job in jobs_of[i]]
                    parts = sb("parts" + tag, [P, NPART, 3, BLK], BF16, tmp)
                    rest = sb("rest" + tag, [P, NPART, BLK], FP32, tmp)
                    s_vp, s_vb = sem("early_values_projected" + tag), sem("early_values_biased" + tag)
                    s_q1, s_q2, s_q3 = (sem(n + tag) for n in ("part1_done", "part2_done", "part3_done"))
                    s_stored = [sem(f"parts_stored{i}" + tag) for i in range(NPART)]
                else:
                    fcol, func, mgate, (w1, w2), (s_w1, s_w2), final = mlp
                    wf1 = sb("wf1" + tag, [P, KC, F], FP32, tmp)
                    wf2 = sb("wf2" + tag, [P, FC, D], FP32, tmp)
                    hid = sb("hid" + tag, [P, FC, BLK], FP32, tmp)
                    s_hid, s_xb, s_out = (sem(n + tag) for n in ("hidden_ready", "mlp_bias_added", "stored"))
                blk = tmp.enter_context(nc.Block())


                def here(b):
                    return 0 <= b < NBLK

                def t_event(b, kc):
                    return KC * b + kc

                def y_event(b, hidden, j):
                    n = 0
                    for i in range(NBLK + 3):
                        for blk_, hid_ in ((i - 1, False), (i - 3, True)):
                            if here(blk_) and (OUT if not hid_ else mlp is not None):
                                if (blk_, hid_) == (b, hidden):
                                    return n + j
                                n += 2

                def transposes(eng, b):
                    for kc in range(KC):
                        n = t_event(b, kc)
                        if n >= 3:
                            eng.wait_ge(s_ev, n - 2)
                        for t in range(TB):
                            if kc == 0:
                                eng.wait_ge(s_h, b * TB + t + 1)
                            last = eng.transpose(ps[:, n % 3, t * P:(t + 1) * P], h[:, b * TB + t, kc * P:(kc + 1) * P], ident[:, :])
                        last.then_inc(s_tp, 1)

                def token_major(eng, b, j, n, terms):
                    if n >= 2:
                        eng.wait_ge(s_yfree, n - 1)
                    for t in range(2):
                        ts = terms(2 * j + t)
                        for i, (lhsT, rhs) in enumerate(ts):
                            last = eng.matmul(ps[:, 3 + n % 2, t * D:(t + 1) * D], lhsT, rhs,
                                              start=(i == 0), stop=(i == len(ts) - 1))
                    last.then_inc(s_y, 1)

                def project_heads(eng, b):
                    if b == NBLK - 1:
                        tail.wait(eng)
                    for j in range(2):
                        token_major(eng, b, j, y_event(b, False, j),
                                    lambda t: [(hT[:, kc, b * BLK + t * P:b * BLK + (t + 1) * P], wt[:, kc, :]) for kc in range(KC)])

                def bank(n):
                    return 5 + n % 3

                @blk.tensor
                def _(eng):
                    eng.wait_ge(s_id, 7)
                    waited = set()
                    if OUT:
                        eng.wait_ge(ld[wload], 16)
                    n = 0
                    for i in range(0, NBLK + 3):
                        if OUT and here(i - 1):
                            project_heads(eng, i - 1)
                        if here(i - 2):
                            transposes(eng, i - 2)
                        b = i - 3
                        if here(b):
                            eng.wait_ge(s_ev, t_event(b, KC - 1) + 1)
                        if projected is not None:
                            for job in jobs_of.get(i, ()):
                                for name, value in job[2]:
                                    if name not in waited:
                                        waited.add(name)
                                        eng.wait_ge(ld[name], value)
                                if n >= 3:
                                    eng.wait_ge(s_pjfree, n - 2)
                                for kc in range(KC):
                                    last = eng.matmul(ps[:, bank(n), 0:job[6]], job[1](kc), job[0][:, kc, job[5][0]:job[5][0] + job[6]],
                                                      start=(kc == 0), stop=(kc == KC - 1))
                                last.then_inc(s_pj, 1)
                                n += 1
                        elif here(b):
                            if b == 0:
                                eng.wait_ge(ld[s_w1], 16)
                            for f in range(FC):
                                if n >= 3:
                                    eng.wait_ge(s_hid, n - 2)
                                for kc in range(KC):
                                    last = eng.matmul(ps[:, bank(n), :], wf1[:, kc, f * P:(f + 1) * P],
                                                      hT[:, kc, b * BLK:(b + 1) * BLK], start=(kc == 0), stop=(kc == KC - 1))
                                last.then_inc(s_pj, 1)
                                n += 1
                            if b == 0:
                                eng.wait_ge(ld[s_w2], 16)
                            eng.wait_ge(s_hid, n)
                            for j in range(2):
                                token_major(eng, b, j, y_event(b, True, j),
                                            lambda t: [(hid[:, f, t * P:(t + 1) * P], wf2[:, f, :]) for f in range(FC)])

                    if values:
                        for tt in range(EARLY):
                            if tt >= 2:
                                eng.wait_ge(s_vb, tt - 1)
                            values.product(eng, tt, 3 + tt % 2).then_inc(s_vp, 1)

                def move_transposed(eng, b):
                    half = b // (NBLK // 2)
                    for kc in range(KC):
                        n = t_event(b, kc)
                        eng.wait_ge(s_tp, n + 1)
                        eng.activation(hT[:, kc, b * BLK:(b + 1) * BLK], ps[:, n % 3, :], ACT.Identity,
                                       bias=shift_at(kc, half), scale=scale_at(kc, half)).then_inc(s_ev, 1)

                @blk.scalar
                def _(eng):
                    eng.wait_ge(ld["cols"], 16)
                    eng.wait_ge(s_id, 7)
                    n = 0
                    for i in range(0, NBLK + 3):
                        if here(i - 1):
                            a, z = (i - 1) * TB, i * TB
                            eng.wait_ge(s_var, z)
                            eng.activation(std[:, a:z], mv[:, a:z, 1], ACT.Sqrt, bias=eps[:, e:e + 1]).then_inc(s_std, 1)
                        if here(i - 2):
                            move_transposed(eng, i - 2)
                        if projected is not None:
                            for job in jobs_of.get(i, ()):
                                _, _, _, col, _, _, nt = job
                                buf = n % NPART
                                if n >= NPART:
                                    eng.wait_ge(s_stored[buf], 16 * (n // NPART))
                                eng.wait_ge(s_pj, n + 1)
                                eng.activation(parts[:, buf, 0, 0:nt], ps[:, bank(n), 0:nt], ACT.Identity,
                                               bias=cols[:, col:col + 1]).then_inc(s_q1, 1)
                                n += 1
                        elif here(i - 3):
                            b = i - 3
                            for f in range(FC):
                                if f == 0 and b >= 1:
                                    eng.wait_ge(s_y, y_event(b - 1, True, 1) + 1)
                                eng.wait_ge(s_pj, n + 1)
                                eng.activation(hid[:, f, :], ps[:, bank(n), :], func,
                                               bias=cols[:, fcol + f:fcol + f + 1]).then_inc(s_hid, 1)
                                n += 1

                def add_product(eng, b, j, n, into, g):
                    t = b * TB + 2 * j
                    v = into[:, t:t + 2, :]
                    eng.wait_ge(s_y, n + 1)
                    p = ps[:, 3 + n % 2, :].rearrange("p (t d) -> p t d", t=2)
                    if g is None:
                        eng.tensor_tensor(v, p, v, ALU.add).then_inc(s_yfree, 1)
                    else:
                        if n >= 2:
                            eng.wait_ge(s_x, n - 1)
                        eng.tensor_tensor(gated_y[:, n % 2, :, :], p, g.to_broadcast([P, 2, D]), ALU.mult).then_inc(s_yfree, 1)
                        eng.wait_ge(s_yfree, n + 1)
                        eng.tensor_tensor(v, v, gated_y[:, n % 2, :, :], ALU.add).then_inc(s_x, 1)

                @blk.vector
                def _(eng):
                    eng.wait_ge(ld["cols"], 16)
                    n = 0
                    for i in range(0, NBLK + 3):
                        b = i - 1
                        if here(b):
                            eng.wait_ge(ld[f"x{b}"], 16)
                            if OUT:
                                if b == 1:
                                    tail.invert(eng)
                                eng.wait_ge(s_b, b + 1)
                                for j in range(2):
                                    add_product(eng, b, j, y_event(b, False, j), src,
                                                None if gk is None else gate[:, b // 2, gk:gk + 1, :])
                                eng.wait_ge(s_yfree if gk is None else s_x, y_event(b, False, 1) + 1)
                            for t in range(b * TB, (b + 1) * TB):
                                eng.bn_stats(st[:, t, :], src[:, t, :]).then_inc(s_stat, 1)
                            for t in range(b * TB, (b + 1) * TB):
                                eng.wait_ge(s_stat, t + 1)
                                eng.bn_aggr(mv[:, t, :], st[:, t, :]).then_inc(s_var, 1)
                            eng.wait_ge(s_std, b + 1)
                            eng.reciprocal(rstd[:, b * TB:(b + 1) * TB], std[:, b * TB:(b + 1) * TB]).then_inc(s_rstd, 1)
                            eng.wait_ge(s_rstd, b + 1)
                            for t in range(b * TB, (b + 1) * TB):
                                eng.tensor_scalar(h[:, t, :], src[:, t, :], mv[:, t, 0:1], rstd[:, t:t + 1],
                                                  ALU.subtract, ALU.mult).then_inc(s_h, 1)
                        if projected is not None:
                            for job in jobs_of.get(i, ()):
                                _, _, _, col, _, _, nt = job
                                buf = n % NPART
                                if n >= NPART:
                                    eng.wait_ge(s_q3, n - NPART + 1)
                                eng.wait_ge(s_q1, n + 1)
                                eng.scalar_tensor_tensor(out=rest[:, buf, 0:nt], in0=ps[:, bank(n), 0:nt],
                                                         scalar=cols[:, col:col + 1], in1=parts[:, buf, 0, 0:nt],
                                                         op0=ALU.add, op1=ALU.subtract).then_inc(s_pjfree, 1)
                                eng.wait_ge(s_pjfree, n + 1)
                                eng.tensor_copy(parts[:, buf, 1, 0:nt], rest[:, buf, 0:nt]).then_inc(s_q2, 1)
                                n += 1
                        elif here(i - 3):
                            b = i - 3
                            eng.wait_ge(s_xb, b + 1)
                            for j in range(2):
                                add_product(eng, b, j, y_event(b, True, j), xs, gate[:, b // 2, 2:3, :] if mgate else None)

                    if values:
                        eng.wait_ge(ld["rows"], 16)
                        for tt in range(EARLY):
                            eng.wait_ge(s_vp, tt + 1)
                            values.move(eng, tt, 3 + tt % 2).then_inc(s_vb, 1)

                @blk.gpsimd
                def _(eng):
                    if not OUT:
                        stage.clear_before(eng)
                    if OUT:
                        eng.wait_ge(ld["rows"], 16)
                        for b in range(NBLK):
                            eng.wait_ge(ld[f"x{b}"], 16)
                            t0, t1 = b * TB, (b + 1) * TB
                            eng.tensor_tensor(src[:, t0:t1, :], xs[:, t0:t1, :], bias(b // 2).to_broadcast([P, TB, D]),
                                              ALU.add).then_inc(s_b, 1)
                        eng.wait_ge(s_b, NBLK)
                        tail.divide(eng)
                        tail.wait(eng)
                    if projected is not None:
                        for i, job in enumerate(job for _, job in jobs):
                            nt, buf = job[6], i % NPART
                            eng.wait_ge(s_q2, i + 1)
                            if i >= NPART:
                                eng.wait_ge(s_stored[buf], 16 * (i // NPART))
                            eng.tensor_tensor(parts[:, buf, 2, 0:nt], rest[:, buf, 0:nt], parts[:, buf, 1, 0:nt],
                                              ALU.subtract).then_inc(s_q3, 1)
                    else:
                        for b in range(NBLK):
                            t0, t1 = b * TB, (b + 1) * TB
                            r = gbias[:, b // 2, 2:3, :] if mgate else rows[:, ROW["ff2_b"]:ROW["ff2_b"] + 1, :]
                            eng.wait_ge(s_h, t1)
                            eng.tensor_tensor(xs[:, t0:t1, :], xs[:, t0:t1, :], r.to_broadcast([P, TB, D]),
                                              ALU.add).then_inc(s_xb, 1)
                    if OUT:
                        stage.clear_before(eng)

                @blk.sync
                def _(eng):
                    if projected is None:
                        eng.dma_start(wf1[:, :, :], chunked(w1)).then_inc(ld[s_w1], 16)
                        eng.dma_start(wf2[:, :, :], chunked(w2)).then_inc(ld[s_w2], 16)
                    if OUT:
                        tail.pack(eng)
                    if projected is not None:
                        stored = [0] * NPART
                        for i, job in enumerate(job for _, job in jobs):
                            _, _, _, _, dst, (_, t0), nt = job
                            buf = i % NPART
                            eng.wait_ge(s_q3, i + 1)
                            eng.dma_start(dst[:, :, t0:t0 + nt], parts[:, buf, :, 0:nt]).then_inc(s_stored[buf], 16)
                            stored[buf] += 16
                        for buf in range(NPART):
                            eng.wait_ge(s_stored[buf], stored[buf])
                    elif final:
                        for n in range(2 * NBLK):
                            eng.wait_ge(s_x, y_event(n // 2, True, n % 2) + 1)
                            eng.dma_start(out.rearrange("(t p) d -> p t d", p=P)[:, 2 * n:2 * n + 2, :],
                                          xs[:, 2 * n:2 * n + 2, :]).then_inc(s_out, 16)
                        eng.wait_ge(s_out, 16 * 2 * NBLK)
            stage.end()

        def attention_stage(a, qd, kd, valued, loads=(), modulated=False):
            stage = Stage()
            sem = stage.sem
            tag = a.name
            s_qk, s_v, s_ones = sem("qk_loaded" + tag), sem("values_ready" + tag), sem("ones_ready" + tag)
            s_a, s_max, s_nm, s_m = (sem(n + tag) for n in ("search_done", "search_bank_free", "maxima_done", "max_parts"))
            s_flip, s_rows, s_laid = sem("maxima_flipped" + tag), sem("max_rows_moved" + tag), sem("max_rows_laid" + tag)
            s_sc, s_ex, s_pv = sem("scores_ready" + tag), sem("exp_done" + tag), sem("pv_done" + tag)
            s_warm = sem("table_loaded" + tag)
            s_vp, s_vb = sem("values_projected" + tag), sem("values_biased" + tag)
            v_tiles = valued.tiles - EARLY
            s_bounce, s_spread = sem("inverses_in_dram" + tag), sem("inverses_spread" + tag)
            s_acc, s_pack, s_inv, s_att = (sem(n + tag) for n in ("accumulator_moved", "heads_packed", "sums_inverted", "heads_divided"))
            PV0 = 2
            MC = 5
            with ExitStack() as tmp:
                Q = sb("Q" + tag, [P, 2, HG, a.NQ], BF16, tmp)
                K = sb("K" + tag, [P, 2, HG, a.NK], BF16, tmp)
                V = sb("V" + tag, [P, a.KT, HG // 2, 4 * DK], FP32, tmp)
                NE = 2 + a.KT % 2
                E = sb("E" + tag, [P, NE, HG, BLK], FP32, tmp)
                mx = sb("mx" + tag, [P, a.NI, a.NKB], FP32, tmp)
                nm = sb("nm" + tag, [P, a.NI], FP32, tmp)
                nr = sb("nr" + tag, [P, 2, a.NI], FP32, tmp)
                mp = sb("mp" + tag, [P, KM, a.NI], BF16, tmp)
                mrow = sb("mrow" + tag, [KM * HG, BLK], BF16, tmp)
                PAIR = [(slice(DK, 3 * DK), 0), (slice(5 * DK, 7 * DK), 2 * DK)]
                SUMS = [(slice(0, 1), 0), (slice(4 * DK - 1, 4 * DK + 1), P // HG), (slice(P - 1, P), 3 * P // HG)]
                PACK = 16 * (len(PAIR) + len(SUMS))
                inv_dram = dram("inverses" + tag, [HG, BLK])

                def heads_at(i, par, b):
                    c, half = (i, 0) if a.J == G else (i % (G // 2), i // (G // 2))
                    return par * GW, c, half * a.NQ + b * BLK

                warm = sb("warm" + tag, [P, 1], FP32, tmp)
                modulation = Modulation(sem, lambda name, shape: sb(name, shape, FP32, tmp), E) if modulated else None
                blk = tmp.enter_context(nc.Block())

                def ebuf(s):
                    return 2 if s == a.KT - 1 and a.KT % 2 else s % 2

                searches = a.KT - a.AHEAD
                AHEAD_CUTS = (0, a.L // 6, a.L // 6 + 5, a.L)
                FLIP = a.L // 3
                INVERT = a.L + (a.NA - a.L) * 4 // searches
                PART_AT = (0, 0, 1, 1, 2)

                def later(v, n):
                    return not isinstance(v, int) or v >= n

                def place(v, k):
                    return k + (later(v, 1) and k >= FLIP)

                def bank(r):
                    return 5 + r % 3

                def wait_use(eng, v, r):
                    if later(v, 1) and r == FLIP:
                        eng.wait_ge(s_rows, v)
                    else:
                        eng.wait_ge(s_max, v * a.NA + r - (later(v, 1) and r > FLIP) + 1)

                def stage_block(u):
                    return u // a.NB, u % a.NB

                def find_max(eng, v, k):
                    j, b = stage_block(v)
                    h, n = k // a.NS, k % a.NS
                    narrow = n >= TB * a.FULL
                    kb = a.FULL if narrow else n % a.FULL
                    for i, qt in enumerate(range(TB) if narrow else (n // a.FULL,)):
                        last = eng.matmul(ps[:, bank(place(v, k)), i * a.KBW[kb]:(i + 1) * a.KBW[kb]],
                                          Q[0:KQ, ds(j % 2, 1), h, ds(b * BLK + qt * P, P)].rearrange("p a t -> p (a t)"),
                                          K[0:KQ, ds(j % 2, 1), h, kb * BLK:kb * BLK + a.KBW[kb]].rearrange("p a t -> p (a t)"),
                                          start=True, stop=True)
                    return last

                def pack(eng, u, i, par, b):
                    p0, c, t0 = heads_at(i, par, b)
                    eng.wait_ge(s_acc, u + 1)
                    for rows_, to in SUMS:
                        n = (rows_.stop - rows_.start) * (P // HG)
                        eng.dma_start(sums[to:to + n, :], O[rows_, :]).then_inc(s_pack, 16)
                    for rows_, to in PAIR:
                        eng.dma_start(hT[p0 + to:p0 + to + 2 * DK, ds(c, 1), ds(t0, BLK)].rearrange("p a t -> p (a t)"),
                                      O[rows_, :]).then_inc(s_pack, 16)
                    eng.wait_ge(s_inv, u + 1)
                    eng.dma_start(inv_dram.rearrange("h (p t) -> (h p) t", t=DK), sums[:, :]).then_inc(s_bounce, 16)
                    eng.wait_ge(s_bounce, 16 * (u + 1))
                    if later(u, 1):
                        eng.wait_ge(s_att, u)
                    eng.dma_start(inverse[p0:p0 + GW, :], inv_dram.rearrange("h (a t) -> h a t", a=1).to_broadcast([HG, DK, BLK]))\
                        .then_inc(s_spread, 16)

                def invert(eng, w):
                    eng.wait_ge(s_pack, PACK * (w + 1))
                    eng.reciprocal(sums[:, :], sums[:, :]).then_inc(s_inv, 1)

                def divide(eng, w, i, par, b, laid=None):
                    p0, c, t0 = heads_at(i, par, b)
                    at = hT[p0:p0 + GW, ds(c, 1), ds(t0, BLK)].rearrange("p a t -> p (a t)")
                    eng.wait_ge(s_spread, 16 * (w + 1))
                    if laid is not None:
                        eng.wait_ge(s_v, a.NVC * laid)
                    if later(w, 1):
                        eng.wait_ge(s_att, w)
                    eng.tensor_tensor(at, at, inverse[p0:p0 + GW, :], ALU.mult).then_inc(s_att, 1)

                @blk.sync
                def _(eng):
                    def load(j, par):
                        for r in range(len(Q_PARTS)):
                            for buf, src, part in ((Q, qd, Q_PARTS[r]), (K, kd, K_PARTS[r])):
                                eng.dma_start(buf[DK * r:DK * (r + 1), par, :, :].rearrange("p a h t -> p (a h) t"),
                                              src[j, :, part, :].rearrange("a (h f) t -> f (a h) t", f=DK)).then_inc(s_qk, 16)

                    def loaded(j):
                        return 16 * 2 * len(Q_PARTS) * (j + 1)

                    def stage_pair(i, last=False):
                        for par in range(2):
                            for b in range(a.NB):
                                j = 2 * i + par
                                if b == a.NB - 1 and not last:
                                    eng.wait_ge(s_sc, (j + 1) * a.NB * a.EV)
                                    eng.wait_ge(s_qk, loaded(j + 1))
                                    load(ds(j + 2, 1), ds(par, 1))
                                if not (last and par == 1 and b == a.NB - 1):
                                    pack(eng, j * a.NB + b, i, par, b)

                    load(ds(0, 1), ds(0, 1))
                    if modulation:
                        modulation.load(eng)
                    eng.wait_ge(s_qk, loaded(0))
                    load(ds(1, 1), ds(1, 1))
                    eng.wait_ge(s_vp, v_tiles)
                    for dst, src, s in loads:
                        eng.dma_start(dst[:, :, :], chunked(src)).then_inc(ld[s], 16)
                    eng.wait_ge(s_vb, v_tiles)
                    stage_pair(0)
                    if a.J > G:
                        with eng.Fori(1, a.J // 2 - 1) as i:
                            stage_pair(i)
                    stage_pair(a.J // 2 - 1, last=True)

                @blk.gpsimd
                def _(eng):
                    stage.clear_before(eng)
                    eng.memset(V[:, :, :, :], 1.0).then_inc(s_ones, 1)
                    eng.wait_ge(s_ones, 1)
                    eng.memset(K[KQ:KQ + KM, :, :, :], 1.0).then_inc(s_ones, 1)
                    eng.wait_ge(s_ones, 2)

                    def values(c, base):
                        k0, k1 = c * a.VC, min((c + 1) * a.VC, a.KT)
                        full = [k for k in range(k0, k1) if a.KW[k] == P]
                        for lo, n, wd in ((k0, len(full), P), (k0 + len(full), k1 - k0 - len(full), a.KW[-1])):
                            if n:
                                last = eng.tensor_copy(V[0:wd, lo:lo + n, :, DK:3 * DK],
                                                       v_all[0:wd, ds(base + lo, n), :].rearrange("p k (h f) -> p k h f", h=2))
                        last.then_inc(s_v, 1)

                    eng.wait_ge(s_vb, v_tiles)
                    for c in range(a.NVC):
                        values(c, 0)
                    if modulation:
                        eng.wait_ge(s_v, a.NVC)
                        modulation.finish(eng)


                    def stage_pair(i, last=False):
                        for par in range(2):
                            j = 2 * i + par
                            for b in range(a.NB):
                                u = j * a.NB + b
                                ahead = b == a.NB - 1 and not (last and par == 1)
                                if ahead:
                                    if later(u, 1):
                                        eng.wait_ge(s_att, u)
                                    for c in range(a.NVC):
                                        eng.wait_ge(s_pv, PV0 + u * a.KT + min((c + 1) * a.VC, a.KT))
                                        values(c, (j + 1) * a.KT)
                                if not (last and par == 1 and b == a.NB - 1):
                                    divide(eng, u, i, par, b, j + 1 + ahead)

                    with eng.Fori(0, a.J // 2 - 1) as i:
                        stage_pair(i)
                    stage_pair(a.J // 2 - 1, last=True)

                @blk.tensor
                def _(eng):
                    def project_values():
                        for n in range(v_tiles):
                            if n >= 4:
                                eng.wait_ge(s_vb, n - 3)
                            valued.product(eng, EARLY + n, n % 4).then_inc(s_vp, 1)

                    def free_bank(v, r):
                        if r >= 3:
                            wait_use(eng, v, r - 3)
                        else:
                            size = place(v - 1, a.NA - 1) + 1
                            wait_use(eng, v - 1, max(n for n in range(size) if n % 3 == r))

                    def flip(w, v, r):
                        eng.wait_ge(s_m, MC * (w + 1))
                        free_bank(v, r)
                        for t in range(TB):
                            last = eng.matmul(ps[0:KM * HG, bank(r), t * P:(t + 1) * P],
                                              mp[:, :, :].rearrange("p m (h t) -> p (m h) t", h=HG)[:, :, t], identb[:, :],
                                              start=True, stop=True)
                        last.then_inc(s_flip, 1)

                    def search(v, k):
                        if k == FLIP and later(v, 1):
                            flip(v - 1, v, FLIP)
                        if later(v, 1) or k >= 3:
                            free_bank(v, place(v, k))
                        find_max(eng, v, k).then_inc(s_a, 1)

                    def scores(u, s, event, p):
                        j, b = u // a.NB, u % a.NB
                        if event is not None:
                            eng.wait_ge(s_ex, event + p - 1)
                        for h in range(2 * p, 2 * p + 2):
                            last = eng.matmul(ps[0:a.KW[s], h, :],
                                              K[0:KQ + KM, ds(j % 2, 1), h, s * P:s * P + a.KW[s]].rearrange("p a t -> p (a t)"),
                                              Q[0:KQ + KM, ds(j % 2, 1), h, ds(b * BLK, BLK)].rearrange("p a t -> p (a t)"),
                                              start=True, stop=True)
                        last.then_inc(s_sc, 1)

                    def weigh(u, s, event, first):
                        if s == 0 and not first:
                            eng.wait_ge(s_acc, u)
                        eng.wait_ge(s_ex, event + 2)
                        if s % a.VC == 0:
                            eng.wait_ge(s_v, (u // a.NB) * a.NVC + s // a.VC + 1)
                        for h in range(HG):
                            last = eng.matmul(ps[32 * h:32 * h + 32, 4, :], V[0:a.KW[s], s, h // 2, h % 2 * 32:h % 2 * 32 + 32], E[0:a.KW[s], ebuf(s), h, :],
                                              start=(s == 0), stop=(s == a.KT - 1))
                        last.then_inc(s_pv, 1)

                    def unit(u, first=False, left=2):
                        n = u * a.EV
                        eng.wait_ge(s_laid, 16 * (u + 1))
                        for s in range(a.KT):
                            if s < searches:
                                lo, hi = (a.L + (a.NA - a.L) * (s + i) // searches for i in range(2))
                                beside = [(u + 1, k) for k in range(lo, hi)] if left >= 1 else []
                            else:
                                lo, hi = AHEAD_CUTS[s - searches:s - searches + 2]
                                beside = [(u + 2, k) for k in range(lo, hi)] if left >= 2 else []
                            if s == searches and left >= 2:
                                eng.wait_ge(s_qk, LOADED * ((u + 2) // a.NB + 1))
                            free = None if first and s == 0 else n
                            scores(u, s, free, 0)
                            for v, k in beside[:1]:
                                search(v, k)
                            scores(u, s, free, 1)
                            for v, k in beside[1:2]:
                                search(v, k)
                            if s > 0:
                                weigh(u, s - 1, before, first)
                            elif not first:
                                weigh(u - 1, a.KT - 1, n - 2, False)
                            for v, k in beside[2:]:
                                search(v, k)
                            if s == searches + 1 and left == 1:
                                flip(u + 1, u + 2, 0)
                            before = n
                            n += 2

                    LOADED = 16 * 2 * len(Q_PARTS)
                    eng.sem_inc(s_pv, PV0)
                    project_values()
                    eng.wait_ge(s_qk, LOADED)
                    if modulation:
                        eng.wait_ge(s_vb, v_tiles)
                    for k in range(a.NA):
                        search(0, k)
                        if modulation and k % 2 and 0 <= k // 2 - 8 < modulation.N:
                            modulation.product(eng, k // 2 - 8)
                    for k in range(a.L):
                        search(1, k)
                    eng.wait_ge(s_vb, v_tiles)
                    if modulation:
                        eng.wait_ge(modulation.s_moved, modulation.N)
                    eng.wait_ge(s_ones, 2)
                    unit(0, first=True)
                    unit(1)
                    with eng.Fori(1, a.U // 2 - 1) as i:
                        unit(2 * i)
                        unit(2 * i + 1)
                    unit(a.U - 2, left=1)
                    unit(a.U - 1, left=0)
                    weigh(a.U - 1, a.KT - 1, a.U * a.EV - 2, False)

                @blk.scalar
                def _(eng):
                    def expose(u, s, event):
                        for p in range(2):
                            eng.wait_ge(s_sc, event + p + 1)
                            if p == 0:
                                eng.wait_ge(s_pv, PV0 + u * a.KT + s - 1)
                            eng.activation(E[0:a.KW[s], ebuf(s), 2 * p:2 * p + 2, :], ps[0:a.KW[s], 2 * p:2 * p + 2, :],
                                           ACT.Exp, scale=SCALE).then_inc(s_ex, 1)

                    def take_rows(u, last=False):
                        eng.wait_ge(s_flip, u + 1)
                        if later(u, 1):
                            eng.wait_ge(s_laid, 16 * u)
                        eng.activation(mrow[:, :], ps[0:KM * HG, bank(0 if last else FLIP), :], ACT.Copy).then_inc(s_rows, 1)

                    def lay_rows(u):
                        j, b = stage_block(u)
                        eng.wait_ge(s_rows, u + 1)
                        eng.dma_start(Q[KQ:KQ + KM, ds(j % 2, 1), :, ds(b * BLK, BLK)].rearrange("p a h t -> p (a h) t"),
                                      mrow[:, :]).then_inc(s_laid, 16)

                    def move_out(u):
                        eng.wait_ge(s_pv, PV0 + (u + 1) * a.KT)
                        if later(u, 1):
                            eng.wait_ge(s_pack, PACK * u)
                        eng.activation(O[:, :], ps[:, 4, :], ACT.Copy).then_inc(s_acc, 1)

                    def unit(u, left=2):
                        n = u * a.EV
                        for s in range(a.KT):
                            if s == a.M_STEP and left >= 1:
                                lay_rows(u + 1)
                            expose(u, s, n)
                            n += 2
                            if s == 0 and later(u, 1):
                                move_out(u - 1)
                            if s == searches + 1 and left >= 1:
                                take_rows(u + 1, last=left == 1)

                    if modulation:
                        modulation.silu(eng)
                        modulation.move(eng)
                    eng.activation(warm[:, :], eps[:, 0:1], ACT.Exp).then_inc(s_warm, 1)
                    take_rows(0)
                    lay_rows(0)
                    unit(0)
                    unit(1)
                    with eng.Fori(1, a.U // 2 - 1) as i:
                        unit(2 * i)
                        unit(2 * i + 1)
                    unit(a.U - 2, left=1)
                    unit(a.U - 1, left=0)
                    move_out(a.U - 1)

                @blk.vector
                def _(eng):
                    def reduce(v, k):
                        h, n = k // a.NS, k % a.NS
                        r = place(v, k)
                        eng.wait_ge(s_a, v * a.NA + k + 1)
                        if n >= TB * a.FULL:
                            i, kb = h * TB, a.FULL
                            of, to = ps[:, bank(r), 0:TB * a.KBW[kb]].rearrange("p (t k) -> p t k", t=TB), mx[:, i:i + TB, kb]
                        else:
                            i, kb = h * TB + n // a.FULL, n % a.FULL
                            of, to = ps[:, bank(r), 0:a.KBW[kb]], mx[:, i, kb:kb + 1]
                        eng.tensor_reduce(to, of, AX.X, ALU.max).then_inc(s_max, 1)

                    def part(w, n):
                        if n == 0:
                            eng.wait_ge(s_nm, w + 1)
                            if later(w, 1):
                                eng.wait_ge(s_flip, w)
                        else:
                            eng.wait_ge(s_m, MC * w + n)
                        if n % 2 == 0:
                            last = eng.tensor_copy(mp[:, n // 2, :], nm[:, :] if n == 0 else nr[:, n // 2 - 1, :])
                        else:
                            last = eng.tensor_tensor(nr[:, n // 2, :], nm[:, :] if n == 1 else nr[:, 0, :], mp[:, n // 2, :], ALU.subtract)
                        last.then_inc(s_m, 1)

                    def maxima(v):
                        for k in range(a.NA):
                            for n in range(MC):
                                if k == PART_AT[n] and later(v, 1):
                                    part(v - 1, n)
                            if k == INVERT and later(v, 2):
                                invert(eng, v - 2)
                            reduce(v, k)
                        eng.wait_ge(s_max, (v + 1) * a.NA)
                        if later(v, 1):
                            eng.wait_ge(s_m, v * MC)
                        eng.tensor_reduce(nm[:, :], mx[:, :, :], AX.X, ALU.max, negate=True).then_inc(s_nm, 1)

                    for n in range(v_tiles):
                        eng.wait_ge(s_vp, n + 1)
                        valued.move(eng, EARLY + n, n % 4).then_inc(s_vb, 1)
                    maxima(0)
                    maxima(1)
                    with eng.Fori(1, a.U // 2) as i:
                        maxima(2 * i)
                        maxima(2 * i + 1)
                    for n in range(MC):
                        part(a.U - 1, n)
                    invert(eng, a.U - 2)
            stage.end()

            class Tail:
                at = (a.U - 1, a.J // 2 - 1, 1, a.NB - 1)

                def pack(eng):
                    pack(eng, *Tail.at)

                def invert(eng):
                    invert(eng, a.U - 1)

                def divide(eng):
                    divide(eng, *Tail.at)

                def wait(eng):
                    eng.wait_ge(s_att, a.U)

            return Tail

        def part_rows(dst, a, c, t0):
            half = t0 // a.NQ if a.J > G else 0
            j = half * G + c * (P // GW)
            return dst[j:j + P // GW].rearrange("j f r t -> (j f) r t"), t0 - half * (S // 2 if a.J > G else 0)

        def projections(n, wt, wload, qcol, swap=0):
            a = attn[n]
            jobs = {}
            for b in range(NBLK):
                jobs[b + 3] = []
                for which, dst in ((0, q_dram[n]), (1, k_dram[n])):
                    for c in range(KC):
                        rows_, t0 = part_rows(dst, a, c, b * BLK)
                        if which and swap:
                            rows_, _ = part_rows(dst, a, c, (b * BLK + S // 2) % S)
                        jobs[b + 3].append((hT, (lambda kc, o=which * D + c * P: wt[:, kc, o:o + P]), ((wload, 16),),
                                            qcol + which * KC + c, rows_, (b * BLK, t0), BLK))
            return jobs

        def cross_projections():
            a = attn[1]
            jobs = {i: [] for i in range(NBLK + 3)}
            wload = (("wcq", 48), ("ctx", 16))
            for b in range((SC + BLK - 1) // BLK):
                nt = min(BLK, SC - b * BLK)
                for c in range(KC):
                    rows_, _ = part_rows(k_dram[1], a, c, 0)
                    jobs[min(b, 2)].append((cT, (lambda kc, o=D + c * P: wcq[:, kc, o:o + P]), wload, COL["ck_b"] + c, rows_,
                                            (b * BLK, b * BLK), nt))
            for b in range(NBLK):
                for c in range(KC):
                    rows_, _ = part_rows(q_dram[1], a, c, 0)
                    jobs[b + 3].append((hT, (lambda kc, o=c * P: wcq[:, kc, o:o + P]), wload, COL["cq_b"] + c, rows_,
                                        (b * BLK, b * BLK), BLK))
            return jobs

        def col(name):
            return lambda kc, half: cols[:, COL[name] + kc:COL[name] + kc + 1]

        def modulation(k):
            return (lambda kc, half: shift[:, 2 * (2 * k + 1) + kc, half:half + 1],
                    lambda kc, half: shift[:, 2 * (2 * k) + kc, half:half + 1])

        def row(name):
            return lambda half: rows[:, ROW[name]:ROW[name] + 1, :]

        def gated_row(k):
            return lambda half: gbias[:, half, k:k + 1, :]

        values = [Values(attn[0], hT, wq, ROW["v_b"], 0), Values(attn[1], cT, wcq, ROW["cv_b"], 0),
                  Values(attn[2], hT, wq, ROW["v2_b"], 0), Values(attn[3], hT, wcq, ROW["cv2_b"], 1)]

        dense_stage("d0", 0, col("ln1_g"), col("ln1_b"),
                    projections(0, wq, "wq", COL["in_b"]), values=values[0])
        tail = attention_stage(attn[0], q_dram[0], k_dram[0], values[0], modulated=True)
        until_modulation.close()
        dense_stage("d1", 0, col("ln2_g"), col("ln2_b"), cross_projections(), attended=(wo, "wo", row("out_b"), None, tail),
                    values=values[1])
        tail = attention_stage(attn[1], q_dram[1], k_dram[1], values[1],
                        ((wq, w["qkv2"], "wq2"), (wo, w["proj2"], "wo2"), (wcq, w["cqkv2"], "wcq2")))
        dense_stage("d2", 0, col("ln3_g"), col("ln3_b"), attended=(wco, "wco", row("co_b"), None, tail),
                    mlp=(COL["ff1_b"], ACT.Gelu, False, (w["ff1"], w["ff2"]), ("wf1", "wf2"), False))

        dense_stage("d3", 1, *modulation(0), projections(2, wq, "wq2", COL["qkv2_b"]), values=values[2])
        tail = attention_stage(attn[2], q_dram[2], k_dram[2], values[2], ((wco, w["cproj2"], "wco2"),))
        dense_stage("d4", 1, *modulation(1), projections(3, wcq, "wcq2", COL["cqkv2_b"], 1),
                    attended=(wo, "wo2", gated_row(0), 0, tail), mid=True, values=values[3])
        tail = attention_stage(attn[3], q_dram[3], k_dram[3], values[3])
        dense_stage("d5", 1, *modulation(2), attended=(wco, "wco2", gated_row(1), 1, tail),
                    mlp=(COL["fc1_b"], ACT.Gelu_apprx_tanh, True, (w["fc12"], w["fc22"]), ("wf12", "wf22"), True))


def kernel(**inputs):
    import numpy as np
    import concourse.bacc as bacc
    from concourse.bass_utils import run_bass_kernel_spmd

    a = {k: np.asarray(v) for k, v in inputs.items()}
    L0, L1 = "L0_xattn_", "L1_xattn_"

    def t(name):
        return np.ascontiguousarray(a[name].T)

    col_at, cols = {}, []
    for name, v in (("ln1_g", a[L0 + "ln1_g"]), ("ln1_b", a[L0 + "ln1_b"]), ("ln2_g", a[L0 + "ln2_g"]),
                    ("ln2_b", a[L0 + "ln2_b"]), ("ln3_g", a[L0 + "ln3_g"]), ("ln3_b", a[L0 + "ln3_b"]),
                    ("in_b", a[L0 + "in_proj_b"]), ("cq_b", a[L0 + "cq_b"]), ("ck_b", a[L0 + "ck_b"]),
                    ("ff1_b", a[L0 + "ff1_b"]), ("qkv2_b", a[L1 + "attn_qkv_b"]), ("cqkv2_b", a[L1 + "crs_qkv_b"]),
                    ("fc1_b", a[L1 + "mlp_fc1_b"]), ("ada_b", a[L1 + "ada_b"])):
        col_at[name] = len(cols)
        cols += list(v.reshape(-1, 128))
    row_at, rows = {}, []
    for name, vs in (("v_b", [a[L0 + "in_proj_b"][512:]]), ("out_b", [a[L0 + "out_proj_b"]]), ("cv_b", [a[L0 + "cv_b"]]),
                     ("co_b", [a[L0 + "co_b"]]), ("ff2_b", [a[L0 + "ff2_b"]]), ("v2_b", [a[L1 + "attn_qkv_b"][512:]]),
                     ("cv2_b", [a[L1 + "crs_qkv_b"][512:]]),
                     ("gate", [a[L1 + "ada_b"][k * 256:(k + 1) * 256] for k in (2, 5, 8)]),
                     ("out2", [a[L1 + "attn_proj_b"], a[L1 + "crs_proj_b"], a[L1 + "mlp_fc2_b"]])):
        row_at[name] = len(rows)
        rows += vs
    arrays = {
        "x": a["x"].reshape(2048, 256), "ctxT": np.ascontiguousarray(a["ctx_1024"][0].T),
        "cols": np.ascontiguousarray(np.stack(cols, 1)), "rows": np.ascontiguousarray(np.stack(rows, 0)),
        "in_proj": t(L0 + "in_proj_w"), "out_proj": t(L0 + "out_proj_w"), "cq": t(L0 + "cq_w"), "ck": t(L0 + "ck_w"),
        "cv": t(L0 + "cv_w"), "co": t(L0 + "co_w"), "ff1": t(L0 + "ff1_w"), "ff2": t(L0 + "ff2_w"),
        "qkv2": a[L1 + "attn_qkv_w"], "proj2": a[L1 + "attn_proj_w"], "cqkv2": a[L1 + "crs_qkv_w"],
        "cproj2": a[L1 + "crs_proj_w"], "fc12": a[L1 + "mlp_fc1_w"], "fc22": a[L1 + "mlp_fc2_w"], "ada": a[L1 + "ada_w"],
    }
    nc = bacc.Bacc("TRN2", target_bir_lowering=False, num_devices=1)
    feeds, w = {}, {}
    for name, v in arrays.items():
        feeds["in_" + name] = np.ascontiguousarray(v)
        w[name] = nc.dram_tensor("in_" + name, v.shape, mybir.dt.from_np(v.dtype), kind="ExternalInput").ap()
    out = nc.dram_tensor("out_0", (2048, 256), FP32, kind="ExternalOutput").ap()
    w["col_at"], w["row_at"] = col_at, row_at
    build(nc, w["x"], w["ctxT"], w, out)
    r = run_bass_kernel_spmd(nc, [feeds], core_ids=[0])
    return r.results[0]["out_0"].reshape(1, 2048, 256)
```
